# Optimizing a Trainium2 kernel written in Bass

```python
import numpy as np
import jax
import jax.numpy as jnp

def _softmax(x, axis=-1):
    return jax.nn.softmax(x, axis=axis)

def _gelu(x):
    return jax.nn.gelu(x, approximate=True)

def _silu(x):
    return jax.nn.silu(x)

def _sigmoid(x):
    return jax.nn.sigmoid(x)

def _layernorm(x, axis=-1, eps=1e-05):
    m = jnp.mean(x, axis=axis, keepdims=True)
    v = jnp.var(x, axis=axis, keepdims=True)
    return (x - m) / jnp.sqrt(v + eps)

def _scatter_add(tgt, idx, src, axis=0):
    return tgt.at[idx].add(src)

def _segment_sum(src, seg, n):
    return jax.ops.segment_sum(src, seg, n)
kernel_name = 'mk_recurrent_d1_jaxref_r4_8a3611'

def setup_inputs(seed: int=0):
    np.random.seed(seed)
    _w = jnp.asarray

    def _L0_attn_setup():
        import jax, jax.numpy as jnp
        import numpy as np
        import math
        B, T, C = (32, 64, 256)
        LAYER_ID, NUM_LAYERS = (12, 24)
        NEG_INF = -1e+38

        def wkv(time_decay, time_first, k, v):
            w = -jnp.exp(time_decay)
            u = time_first
            kT = jnp.swapaxes(k, 0, 1)
            vT = jnp.swapaxes(v, 0, 1)

            def step(carry, kv):
                p, q, o = carry
                kt, vt = kv
                no = jnp.maximum(o, u + kt)
                A = jnp.exp(o - no)
                Bc = jnp.exp(u + kt - no)
                y = (A * p + Bc * vt) / (A * q + Bc)
                no2 = jnp.maximum(w + o, kt)
                A2 = jnp.exp(w + o - no2)
                B2 = jnp.exp(kt - no2)
                return ((A2 * p + B2 * vt, A2 * q + B2, no2), y)
            init = (jnp.zeros((k.shape[0], k.shape[2]), k.dtype), jnp.zeros((k.shape[0], k.shape[2]), k.dtype), jnp.full((k.shape[0], k.shape[2]), NEG_INF, k.dtype))
            _, yT = jax.lax.scan(step, init, (kT, vT))
            return jnp.swapaxes(yT, 0, 1)
        key = jax.random.key(seed)
        ks = jax.random.split(key, 5)
        x = jax.random.normal(ks[0], (B, T, C), dtype=jnp.float32)
        r01 = LAYER_ID / (NUM_LAYERS - 1)
        r10 = 1.0 - LAYER_ID / NUM_LAYERS
        h = jnp.arange(C, dtype=jnp.float32)
        time_decay = -5.0 + 8.0 * (h / (C - 1)) ** (0.7 + 1.3 * r01)
        tf = (jnp.arange(C) + 1) % 3 - 1
        time_first = jnp.full((C,), math.log(0.3), jnp.float32) + 0.5 * tf.astype(jnp.float32)
        xr = (jnp.arange(C, dtype=jnp.float32) / C)[None, None, :]
        time_mix_k = xr ** r10
        time_mix_v = xr ** r10 + 0.3 * r01
        time_mix_r = xr ** (0.5 * r10)
        s = 1.0 / math.sqrt(C)
        Wk = jax.random.normal(ks[1], (C, C), jnp.float32) * s
        Wv = jax.random.normal(ks[2], (C, C), jnp.float32) * s
        Wr = jax.random.normal(ks[3], (C, C), jnp.float32) * s
        Wo = jax.random.normal(ks[4], (C, C), jnp.float32) * s
        return {'x': x, 'time_decay': time_decay, 'time_first': time_first, 'time_mix_k': time_mix_k, 'time_mix_v': time_mix_v, 'time_mix_r': time_mix_r, 'Wk': Wk, 'Wv': Wv, 'Wr': Wr, 'Wo': Wo}
    _L0_attn_in = _L0_attn_setup()

    def _L0_ffn_setup():
        import jax, jax.numpy as jnp
        import numpy as np
        B, S, DIM = (4, 1024, 256)
        BASE_COUPLING = 0.1
        NUM_CYCLES = 3

        def _gelu(x):
            return jax.nn.gelu(x, approximate=False)

        def _coupling_net(h, w1, b1, w2, b2, w3, b3, w4, b4):
            h = _gelu(h @ w1 + b1)
            h = _gelu(h @ w2 + b2)
            h = _gelu(h @ w3 + b3)
            return jax.nn.sigmoid(h @ w4 + b4)

        def _global_net(h, w1, b1, w2, b2, w3, b3):
            h = _gelu(h @ w1 + b1)
            h = _gelu(h @ w2 + b2)
            return jax.nn.sigmoid(h @ w3 + b3)

        def _twist(x):
            o_r, o_i, p_r, p_i = jnp.split(x, 4, axis=-1)
            return jnp.concatenate([p_r, -p_i, -o_r, o_i], axis=-1)
        key = jax.random.key(seed)
        ks = jax.random.split(key, 9)
        d = DIM

        def w(k, fan_in, fan_out):
            return jax.random.normal(k, (fan_in, fan_out), dtype=jnp.float32) / np.sqrt(fan_in).astype(np.float32)
        inp = {'x': jax.random.normal(ks[0], (B, S, d), dtype=jnp.float32)}
        cn_dims = [(d, d), (d, d // 2), (d // 2, d // 4), (d // 4, 1)]
        for i, (a, b) in enumerate(cn_dims):
            inp[f'cn_w{i + 1}'] = w(ks[1 + i], a, b)
            inp[f'cn_b{i + 1}'] = jnp.zeros((b,), dtype=jnp.float32)
        gc_dims = [(d, d // 2), (d // 2, d // 4), (d // 4, 1)]
        for i, (a, b) in enumerate(gc_dims):
            inp[f'gc_w{i + 1}'] = w(ks[5 + i], a, b)
            inp[f'gc_b{i + 1}'] = jnp.zeros((b,), dtype=jnp.float32)
        inp['adaptive_range'] = jnp.full((1,), 0.2, dtype=jnp.float32)
        return inp
    _L0_ffn_in = _L0_ffn_setup()
    _d = {'L0_attn_x': _L0_attn_in['x'], 'L0_attn_time_decay': _L0_attn_in['time_decay'], 'L0_attn_time_first': _L0_attn_in['time_first'], 'L0_attn_time_mix_k': _L0_attn_in['time_mix_k'], 'L0_attn_time_mix_v': _L0_attn_in['time_mix_v'], 'L0_attn_time_mix_r': _L0_attn_in['time_mix_r'], 'L0_attn_Wk': _L0_attn_in['Wk'], 'L0_attn_Wv': _L0_attn_in['Wv'], 'L0_attn_Wr': _L0_attn_in['Wr'], 'L0_attn_Wo': _L0_attn_in['Wo'], 'L0_ffn_cn_w1': _L0_ffn_in['cn_w1'], 'L0_ffn_cn_b1': _L0_ffn_in['cn_b1'], 'L0_ffn_cn_w2': _L0_ffn_in['cn_w2'], 'L0_ffn_cn_b2': _L0_ffn_in['cn_b2'], 'L0_ffn_cn_w3': _L0_ffn_in['cn_w3'], 'L0_ffn_cn_b3': _L0_ffn_in['cn_b3'], 'L0_ffn_cn_w4': _L0_ffn_in['cn_w4'], 'L0_ffn_cn_b4': _L0_ffn_in['cn_b4'], 'L0_ffn_gc_w1': _L0_ffn_in['gc_w1'], 'L0_ffn_gc_b1': _L0_ffn_in['gc_b1'], 'L0_ffn_gc_w2': _L0_ffn_in['gc_w2'], 'L0_ffn_gc_b2': _L0_ffn_in['gc_b2'], 'L0_ffn_gc_w3': _L0_ffn_in['gc_w3'], 'L0_ffn_gc_b3': _L0_ffn_in['gc_b3'], 'L0_ffn_adaptive_range': _L0_ffn_in['adaptive_range']}
    _x0 = _d['L0_attn_x']
    _d['L0_attn_x'] = jax.random.normal(jax.random.fold_in(jax.random.key(seed), 1), (1, 4096, 256), dtype=_x0.dtype)
    del _x0
    return _d

def reference(L0_attn_x, L0_attn_time_decay, L0_attn_time_first, L0_attn_time_mix_k, L0_attn_time_mix_v, L0_attn_time_mix_r, L0_attn_Wk, L0_attn_Wv, L0_attn_Wr, L0_attn_Wo, L0_ffn_cn_w1, L0_ffn_cn_b1, L0_ffn_cn_w2, L0_ffn_cn_b2, L0_ffn_cn_w3, L0_ffn_cn_b3, L0_ffn_cn_w4, L0_ffn_cn_b4, L0_ffn_gc_w1, L0_ffn_gc_b1, L0_ffn_gc_w2, L0_ffn_gc_b2, L0_ffn_gc_w3, L0_ffn_gc_b3, L0_ffn_adaptive_range):

    def _L0_attn_ref(x, time_decay, time_first, time_mix_k, time_mix_v, time_mix_r, Wk, Wv, Wr, Wo):
        import jax, jax.numpy as jnp
        import numpy as np
        import math
        B, T, C = (32, 64, 256)
        LAYER_ID, NUM_LAYERS = (12, 24)
        NEG_INF = -1e+38

        def wkv(time_decay, time_first, k, v):
            w = -jnp.exp(time_decay)
            u = time_first
            kT = jnp.swapaxes(k, 0, 1)
            vT = jnp.swapaxes(v, 0, 1)

            def step(carry, kv):
                p, q, o = carry
                kt, vt = kv
                no = jnp.maximum(o, u + kt)
                A = jnp.exp(o - no)
                Bc = jnp.exp(u + kt - no)
                y = (A * p + Bc * vt) / (A * q + Bc)
                no2 = jnp.maximum(w + o, kt)
                A2 = jnp.exp(w + o - no2)
                B2 = jnp.exp(kt - no2)
                return ((A2 * p + B2 * vt, A2 * q + B2, no2), y)
            init = (jnp.zeros((k.shape[0], k.shape[2]), k.dtype), jnp.zeros((k.shape[0], k.shape[2]), k.dtype), jnp.full((k.shape[0], k.shape[2]), NEG_INF, k.dtype))
            _, yT = jax.lax.scan(step, init, (kT, vT))
            return jnp.swapaxes(yT, 0, 1)
        xx = jnp.pad(x, ((0, 0), (1, 0), (0, 0)))[:, :-1, :]
        xk = x * time_mix_k + xx * (1.0 - time_mix_k)
        xv = x * time_mix_v + xx * (1.0 - time_mix_v)
        xr = x * time_mix_r + xx * (1.0 - time_mix_r)
        k = jnp.einsum('btc,dc->btd', xk, Wk)
        v = jnp.einsum('btc,dc->btd', xv, Wv)
        r = jnp.einsum('btc,dc->btd', xr, Wr)
        sr = jax.nn.sigmoid(r)
        rwkv = sr * wkv(time_decay, time_first, k, v)
        return jnp.einsum('btc,dc->btd', rwkv, Wo)

    def _L0_ffn_ref(x, cn_w1, cn_b1, cn_w2, cn_b2, cn_w3, cn_b3, cn_w4, cn_b4, gc_w1, gc_b1, gc_w2, gc_b2, gc_w3, gc_b3, adaptive_range):
        import jax, jax.numpy as jnp
        import numpy as np
        B, S, DIM = (4, 1024, 256)
        BASE_COUPLING = 0.1
        NUM_CYCLES = 3

        def _gelu(x):
            return jax.nn.gelu(x, approximate=False)

        def _coupling_net(h, w1, b1, w2, b2, w3, b3, w4, b4):
            h = _gelu(h @ w1 + b1)
            h = _gelu(h @ w2 + b2)
            h = _gelu(h @ w3 + b3)
            return jax.nn.sigmoid(h @ w4 + b4)

        def _global_net(h, w1, b1, w2, b2, w3, b3):
            h = _gelu(h @ w1 + b1)
            h = _gelu(h @ w2 + b2)
            return jax.nn.sigmoid(h @ w3 + b3)

        def _twist(x):
            o_r, o_i, p_r, p_i = jnp.split(x, 4, axis=-1)
            return jnp.concatenate([p_r, -p_i, -o_r, o_i], axis=-1)
        global_context = x.mean(axis=1, keepdims=True)
        gf = _global_net(global_context, gc_w1, gc_b1, gc_w2, gc_b2, gc_w3, gc_b3)
        out = x
        for _ in range(NUM_CYCLES):
            tf = _coupling_net(out, cn_w1, cn_b1, cn_w2, cn_b2, cn_w3, cn_b3, cn_w4, cn_b4)
            combined = 0.7 * gf + 0.3 * tf
            coupling = BASE_COUPLING + adaptive_range * (combined - 0.5) * 2.0
            out = out + coupling * _twist(out)
        return out
    x = L0_attn_x
    xn = _layernorm(x, axis=-1)
    s = _L0_attn_ref(xn, L0_attn_time_decay, L0_attn_time_first, L0_attn_time_mix_k, L0_attn_time_mix_v, L0_attn_time_mix_r, L0_attn_Wk, L0_attn_Wv, L0_attn_Wr, L0_attn_Wo)
    g = _silu(_L0_ffn_ref(xn, L0_ffn_cn_w1, L0_ffn_cn_b1, L0_ffn_cn_w2, L0_ffn_cn_b2, L0_ffn_cn_w3, L0_ffn_cn_b3, L0_ffn_cn_w4, L0_ffn_cn_b4, L0_ffn_gc_w1, L0_ffn_gc_b1, L0_ffn_gc_w2, L0_ffn_gc_b2, L0_ffn_gc_w3, L0_ffn_gc_b3, L0_ffn_adaptive_range))
    x = x + s * g
    return x

_drawn_inputs = setup_inputs


def setup_inputs(seed=0):
    import zlib

    import numpy as np

    out = dict(_drawn_inputs(seed))
    spreads = {'L0_ffn_cn_b1': (0.0, 2.0),
     'L0_ffn_cn_b2': (0.0, 2.0),
     'L0_ffn_cn_b3': (0.0, 2.0),
     'L0_ffn_gc_b1': (0.0, 0.8),
     'L0_ffn_gc_b2': (0.0, 0.8)}
    factors = {'L0_attn_time_first': 68.456,
     'L0_attn_time_mix_r': 3.284,
     'L0_ffn_cn_w1': 8.0,
     'L0_ffn_cn_w2': 8.0,
     'L0_ffn_cn_w3': 8.0,
     'L0_ffn_cn_w4': 8.0,
     'L0_ffn_gc_w1': 64.0,
     'L0_ffn_gc_w2': 64.0,
     'L0_ffn_gc_w3': 8.0}
    for name, (base, spread) in spreads.items():
        noise = np.random.default_rng([zlib.crc32(name.encode()), seed]).standard_normal(out[name].shape)
        drawn = base * np.exp(spread * noise) if base else spread * noise
        out[name] = jnp.asarray(drawn.astype(out[name].dtype))
    for name, factor in factors.items():
        out[name] = (out[name] * factor).astype(out[name].dtype)
    return out
```

```python
from contextlib import ExitStack

import concourse.bass as bass
from concourse import mybir

F32 = mybir.dt.float32
ALU = mybir.AluOpType
ACT = mybir.ActivationFunctionType
AX_X = mybir.AxisListType.X

P = 128
EXP_LN_SET = "natural_log_exp_and_others"
LN_EPS = 1e-5
NEG_INF = -1e38
BASE_COUPLING = 0.1
WKV_LAG = 2
OUT_LAG = 3
CYCLES = 3

DECAY, FIRST, MIX, CN_B1, CN_B2, CN_B3, CN_B4, GC_B1, GC_B2, GC_B3, RANGE, SIGN, NVEC = (
    0, 2, 4, 10, 12, 13, 14, 15, 16, 17, 18, 19, 20)


class Slot:

    def __init__(self, tiles, base, reg=None):
        self.tiles, self.base, self.reg = tiles, base, reg

    def live(self, lag):
        return self.reg is not None or 0 <= self.base - lag < self.tiles

    def count(self, lag, per_tile, k=0):
        const = per_tile * (self.base - lag) + k
        if self.reg is None:
            return max(0, min(const, per_tile * self.tiles))
        assert const > 0
        return self.reg * per_tile + const

    def tile(self, lag):
        return self.base - lag if self.reg is None else self.reg + (self.base - lag)


def rwkv_coupled_ffn(nc, x, vec, wk_t, wv_t, wr_t, wo_t, cn_w1, cn_w2, cn_w3, cn_w4, gc_w1, gc_w2, gc_w3, out):
    T, C = x.shape
    M = C // P
    TN = 512
    NT = T // TN
    SUB = TN // P
    D2 = cn_w2.shape[1]
    D3 = cn_w3.shape[1]
    SLOTS = NT + OUT_LAG
    STEADY = (OUT_LAG + 1, NT)
    assert M == 2 and D2 == P and D3 == 64 and SUB * C == 2 * TN

    x_tiles = x.rearrange("(g s p) c -> g p s c", s=SUB, p=P)
    out_tiles = out.rearrange("(g s p) c -> g p s c", s=SUB, p=P)

    with ExitStack() as ctx:
        def sb(name, *shape):
            return ctx.enter_context(nc.sbuf_tensor(name, [P, *shape], F32))

        def sem(name):
            return ctx.enter_context(nc.semaphore(name))

        vecs = sb("vecs", NVEC)
        w_kvr = sb("w_kvr", 3, M, C)
        w_o = sb("w_o", M, C)
        w_c1 = sb("w_c1", M, C)
        w_c2 = sb("w_c2", M, D2)
        w_c3 = sb("w_c3", D3)
        w_c4 = sb("w_c4", P)
        w_g1 = sb("w_g1", M, D2)
        w_g2 = sb("w_g2", D3)
        w_g3 = sb("w_g3", P)
        ident = sb("ident", P)
        decay_pos = sb("decay_pos", M)
        decay = sb("decay", M)
        neg_first = sb("neg_first", M)
        half_b4 = sb("half_b4", 1)
        half_g3 = sb("half_g3", 1)
        eps = sb("eps", 1)
        beta = sb("beta", 1)
        alpha = sb("alpha", 1)
        range_sign = sb("range_sign", 1)
        base_sign = sb("base_sign", 1)
        stats = sb("stats", 2, SUB, 6)
        meanvar = sb("meanvar", NT, SUB, 2)
        std = sb("std", NT, SUB)
        rstd = sb("rstd", NT, SUB)
        shift = sb("shift", NT, SUB)
        tile_sums = sb("tile_sums", M, NT)
        ctx_sum = sb("ctx_sum", M)
        ctx_mean = sb("ctx_mean", M)
        g_h1 = sb("g_h1", 1)
        g_h2 = sb("g_h2", 1)
        g_tanh = sb("g_tanh", 1)
        xt = sb("xt", M, 1 + T)
        diff = sb("diff", M, TN)
        mixed = sb("mixed", 3, M, TN)
        kv = sb("kv", 2, M, TN)
        r_tanh = sb("r_tanh", M, TN)
        rel = sb("rel", M, TN)
        ex = sb("ex", 4, M, TN)
        STATE_Y, TOKEN_Y, STATE_W, TOKEN_W = range(4)
        opq = sb("opq", 3, M, 1 + TN)
        b2v = sb("b2v", M, TN)
        aq = sb("aq", M, TN)
        ap_ = sb("ap", M, TN)
        den = sb("den", M, TN)
        num = sb("num", M, TN)
        rec = sb("rec", M, TN)
        y = sb("y", M, TN)
        h1 = [sb(f"h1_{c}", M, TN) for c in range(CYCLES)]
        h2 = [sb(f"h2_{c}", TN) for c in range(CYCLES)]
        h3 = [sb(f"h3_{c}", TN) for c in range(CYCLES)]
        tanh_c = [sb(f"tanh_{c}", TN) for c in range(CYCLES)]
        coup = [sb(f"coup_{c}", TN) for c in range(CYCLES)]
        turned = [sb(f"turned_{i}", M, TN) for i in range(2)]
        state = [sb(f"state_{c}", M, TN) for c in range(CYCLES)]
        o_tanh = sb("o_tanh", SUB, C)
        gate = sb("gate", SUB, C)
        gated = sb("gated", SUB, C)
        resid = sb("resid", SUB, C)
        XS = 4
        x_stage = ex[:, :, :, :].rearrange("p a m t -> p a (m t)").rearrange("p a (s c) -> p a s c", c=C)
        xn_stage = kv[:, :, :, :].rearrange("p a m t -> p a (m t)").rearrange("p a (s c) -> p a s c", c=C)

        ps = ctx.enter_context(nc.psum_tensor("ps", [P, 8, TN], F32))
        KVR_BANK = 2 * CYCLES
        tok = ps[:, KVR_BANK:KVR_BANK + 2, :].rearrange("p b t -> p (b t)").rearrange("p (s c) -> p s c", c=C)

        s_vec = sem("vec_loaded")
        s_wt = sem("weights_loaded")
        s_x = [sem(f"x_loaded_{i}") for i in range(XS)]
        s_zero = sem("ident_zeroed")
        s_ident = sem("ident_ready")
        s_init = sem("carries_ready")
        s_decay = sem("decay_ready")
        s_const = sem("constants_ready")
        s_eps = sem("eps_ready")
        s_stat = sem("stats_done")
        s_mv = sem("meanvar_done")
        s_std = sem("std_done")
        s_rstd = sem("rstd_done")
        s_shift = sem("shift_done")
        s_xn_v = sem("xn_vector_done")
        s_xn_s = sem("xn_scalar_done")
        s_xt = sem("xt_transposed")
        s_xe = sem("xt_stored")
        s_sum = sem("context_summed")
        s_mean = sem("context_mean_done")
        s_gp = sem("global_layer_done")
        s_ga = sem("global_act_done")
        s_alpha = sem("alpha_ready")
        s_diff = sem("diff_done")
        s_mix = sem("mix_done")
        s_kvr = sem("kvr_done")
        s_kv = sem("kv_stored")
        s_rt = sem("r_tanh_done")
        s_o = sem("o_scanned")
        s_rel = sem("rel_done")
        s_relu = sem("output_exponents_done")
        s_arg = sem("state_exponents_done")
        s_ex = sem("exps_done")
        s_b2v = sem("b2v_done")
        s_q = sem("q_scanned")
        s_p = sem("p_scanned")
        s_aq = sem("aq_done")
        s_ap = sem("ap_done")
        s_den = sem("den_done")
        s_bv = sem("bv_done")
        s_num = sem("num_done")
        s_numr = sem("num_times_r_done")
        s_carry = sem("carry_done")
        s_ln = sem("ln_done")
        s_rec = sem("rec_done")
        s_y = sem("y_done")
        s_h1 = [sem(f"h1_pre_{c}") for c in range(CYCLES)]
        s_h2 = [sem(f"h2_pre_{c}") for c in range(CYCLES)]
        s_h3 = [sem(f"h3_pre_{c}") for c in range(CYCLES)]
        s_lg = [sem(f"logit_{c}") for c in range(CYCLES)]
        s_g1 = [sem(f"h1_done_{c}") for c in range(CYCLES)]
        s_g2 = [sem(f"h2_done_{c}") for c in range(CYCLES)]
        s_g3 = [sem(f"h3_done_{c}") for c in range(CYCLES)]
        s_th = [sem(f"tanh_done_{c}") for c in range(CYCLES)]
        s_cs = [sem(f"coupling_done_{c}") for c in range(CYCLES)]
        s_mul = [sem(f"turn_done_{c}") for c in range(CYCLES)]
        s_st = [sem(f"state_done_{c}") for c in range(CYCLES)]
        s_tp = sem("out_transposed")
        s_ot = sem("o_tanh_done")
        s_gate = sem("gate_done")
        s_proj = sem("out_projected")
        s_z = sem("gated_done")
        s_xr = sem("residual_loaded")
        s_add = sem("sum_done")
        s_out = sem("out_stored")

        peeled_first = [Slot(NT, j) for j in range(STEADY[0])]
        peeled_last = [Slot(NT, j) for j in range(STEADY[1], SLOTS)]

        def run_slots(eng, slot_body):
            for slot in peeled_first:
                slot_body(slot)
            with eng.Fori(0, STEADY[1] - STEADY[0]) as i:
                slot_body(Slot(NT, STEADY[0], i))
            for slot in peeled_last:
                slot_body(slot)

        def xt_cols(slot, lag, first=1):
            if slot.reg is None:
                at = (slot.base - lag) * TN + first
                return xt[:, :, at:at + TN]
            return xt[:, :, bass.ds(slot.reg * TN + ((slot.base - lag) * TN + first), TN)]

        def source(slot, cycle, lag):
            return xt_cols(slot, lag) if cycle == 0 else state[cycle - 1][:, :, :]

        block = ctx.enter_context(nc.Block())

        @block.sync
        def _(sp):
            sp.dma_start(vecs[:, :], vec).then_inc(s_vec, 16)
            for g in range(NT):
                if g >= XS:
                    sp.wait_ge(s_xn_v, 2 * (g - XS) + 2)
                    sp.wait_ge(s_xn_s, 2 * (g - XS) + 2)
                sp.dma_start(x_stage[:, g % XS, :, :], x_tiles[g]).then_inc(s_x[g % XS], 16)

            def slot_body(s):
                if s.live(OUT_LAG):
                    sp.wait_ge(s_out, s.count(OUT_LAG, 16))
                    sp.dma_start(resid[:, :, :], x_tiles[s.tile(OUT_LAG)]).then_inc(s_xr, 16)
                    sp.wait_ge(s_add, s.count(OUT_LAG, 1, 1))
                    sp.dma_start(out_tiles[s.tile(OUT_LAG)], resid[:, :, :]).then_inc(s_out, 16)
            run_slots(sp, slot_body)
            sp.wait_ge(s_out, 16 * NT)

        @block.gpsimd
        def _(pool):
            nc.gpsimd.memset(ident[:, :], 0.0).then_inc(s_zero, 1)
            pool.wait_ge(s_zero, 1)
            nc.gpsimd.affine_select(out=ident[:, :], in_=ident[:, :], compare_op=ALU.not_equal, fill=1.0,
                                    base=0, pattern=[[-1, P]], channel_multiplier=1).then_inc(s_ident, 1)
            nc.gpsimd.memset(xt[:, :, 0:1], 0.0).then_inc(s_init, 1)
            nc.gpsimd.memset(opq[:, 0, :, 0:1], NEG_INF).then_inc(s_init, 1)
            nc.gpsimd.memset(opq[:, 1:3, :, 0:1], 0.0).then_inc(s_init, 1)
            pool.wait_ge(s_init, 3)
            pool.wait_ge(s_xe, M * NT)

            def slot_body(s):
                if s.live(1):
                    pool.wait_ge(s_mix, s.count(1, 3 * M))
                    nc.gpsimd.tensor_tensor(diff[:, :, :], xt_cols(s, 1), xt_cols(s, 1, 0),
                                            ALU.subtract).then_inc(s_diff, 1)
                if s.live(OUT_LAG):
                    pool.wait_ge(s_xr, s.count(OUT_LAG, 16, 16))
                    pool.wait_ge(s_z, s.count(OUT_LAG, 2, 2))
                    nc.gpsimd.tensor_tensor(resid[:, :, :], gated[:, :, :], resid[:, :, :],
                                            ALU.add).then_inc(s_add, 1)
            run_slots(pool, slot_body)

        @block.scalar
        def _(act):
            for dst, src in ((w_c1[:, :, :], cn_w1.rearrange("(k p) n -> p k n", p=P)),
                             (w_g1[:, :, :], gc_w1.rearrange("(k p) n -> p k n", p=P)),
                             (w_g2[:, :], gc_w2), (w_g3[0:D3, :], gc_w3),
                             (w_c2[:, :, :], cn_w2.rearrange("(k p) n -> p k n", p=P)),
                             (w_c3[:, :], cn_w3), (w_c4[0:D3, :], cn_w4),
                             (w_kvr[:, 0, :, :], wk_t.rearrange("(k p) n -> p k n", p=P)),
                             (w_kvr[:, 1, :, :], wv_t.rearrange("(k p) n -> p k n", p=P)),
                             (w_kvr[:, 2, :, :], wr_t.rearrange("(k p) n -> p k n", p=P)),
                             (w_o[:, :, :], wo_t.rearrange("(k p) n -> p k n", p=P))):
                act.dma_start(dst, src).then_inc(s_wt, 16)
            act.wait_ge(s_vec, 16)
            nc.scalar.activation(decay_pos[:, :], vecs[:, DECAY:DECAY + M], ACT.Exp).then_inc(s_decay, 1)

            def normalise(g):
                act.wait_ge(s_shift, g + 1)
                if g >= 2:
                    act.wait_ge(s_xt, M * (g - 1))
                for k in range(SUB // 2, SUB):
                    nc.scalar.activation(xn_stage[:, g % 2, k, :], x_stage[:, g % XS, k, :], ACT.Identity,
                                         bias=shift[:, g, k:k + 1], scale=rstd[:, g, k:k + 1]
                                         ).then_inc(s_xn_s, 1)

            def store_xt(g):
                for m in range(M):
                    act.wait_ge(s_xt, M * g + m + 1)
                    nc.scalar.activation(xt[:, m, 1 + g * TN:1 + (g + 1) * TN], ps[:, 2 * (g % 4) + m, :],
                                         ACT.Identity, accum_out=tile_sums[:, m, g:g + 1]).then_inc(s_xe, 1)

            act.wait_ge(s_eps, 1)
            for g in range(NT):
                act.wait_ge(s_mv, SUB * (g + 1))
                nc.scalar.activation(std[:, g, :], meanvar[:, g, :, 1], ACT.Sqrt,
                                     bias=eps[:, :]).then_inc(s_std, 1)
                normalise(g)
                if g >= 1:
                    store_xt(g - 1)
            store_xt(NT - 1)

            act.wait_ge(s_gp, 1)
            nc.scalar.activation(g_h1[:, :], ps[:, KVR_BANK, 0:1], ACT.Gelu,
                                 bias=vecs[:, GC_B1:GC_B1 + 1]).then_inc(s_ga, 1)
            act.wait_ge(s_gp, 2)
            nc.scalar.activation(g_h2[0:D3, :], ps[0:D3, KVR_BANK, 1:2], ACT.Gelu,
                                 bias=vecs[0:D3, GC_B2:GC_B2 + 1]).then_inc(s_ga, 1)
            act.wait_ge(s_gp, 3)
            nc.scalar.activation(g_tanh[:, :], ps[:, KVR_BANK, 2:3], ACT.Tanh, scale=0.5,
                                 bias=half_g3[:, :]).then_inc(s_ga, 1)

            act.wait_ge(s_alpha, 2)
            act.wait_ge(s_const, 8)

            def gelu1(s, c):
                if s.live(c):
                    for m in range(M):
                        act.wait_ge(s_h1[c], s.count(c, M, m + 1))
                        nc.scalar.activation(h1[c][:, m, :], ps[:, 2 * c + m, :], ACT.Gelu,
                                             bias=vecs[:, CN_B1 + m:CN_B1 + m + 1]).then_inc(s_g1[c], 1)

            def gelu2(s, c):
                if s.live(c):
                    act.wait_ge(s_h2[c], s.count(c, 1, 1))
                    nc.scalar.activation(h2[c][:, :], ps[:, 2 * c, :], ACT.Gelu,
                                         bias=vecs[:, CN_B2:CN_B2 + 1]).then_inc(s_g2[c], 1)

            def gelu3(s, c):
                if s.live(c):
                    act.wait_ge(s_h3[c], s.count(c, 1, 1))
                    nc.scalar.activation(h3[c][0:D3, :], ps[0:D3, 2 * c + 1, :], ACT.Gelu,
                                         bias=vecs[0:D3, CN_B3:CN_B3 + 1]).then_inc(s_g3[c], 1)

            def tanh_logit(s, c):
                if s.live(c):
                    act.wait_ge(s_lg[c], s.count(c, 1, 1))
                    nc.scalar.activation(tanh_c[c][:, :], ps[:, 2 * c, :], ACT.Tanh, scale=0.5,
                                         bias=half_b4[:, :]).then_inc(s_th[c], 1)

            def coupling(s, c):
                if s.live(c):
                    act.wait_ge(s_th[c], s.count(c, 1, 1))
                    act.wait_ge(s_mul[c], s.count(c, 1))
                    nc.scalar.activation(coup[c][:, :], tanh_c[c][:, :], ACT.Identity, scale=beta[:, :],
                                         bias=alpha[:, :]).then_inc(s_cs[c], 1)

            def slot_body(s):
                wkv, o = s.live(WKV_LAG), s.live(OUT_LAG)
                if wkv or o:
                    nc.scalar.preload_act_table_set(EXP_LN_SET)
                if o:
                    act.wait_ge(s_den, s.count(OUT_LAG, 1, 1))
                    act.wait_ge(s_y, s.count(OUT_LAG, 1))
                    nc.scalar.activation(rec[:, :, :], den[:, :, :], ACT.Ln).then_inc(s_ln, 1)
                if wkv:
                    for m in range(M):
                        act.wait_ge(s_kvr, s.count(WKV_LAG, 6, m + 1))
                        act.wait_ge(s_rel, s.count(WKV_LAG, 1))
                        nc.scalar.copy(kv[:, 0, m, :], ps[:, KVR_BANK + m, :]).then_inc(s_kv, 1)
                if o:
                    act.wait_ge(s_ln, s.count(OUT_LAG, 1, 1))
                    nc.scalar.activation(rec[:, :, :], rec[:, :, :], ACT.Exp, scale=-1.0).then_inc(s_rec, 1)
                if wkv:
                    for m in range(M):
                        act.wait_ge(s_kvr, s.count(WKV_LAG, 6, M + m + 1))
                        act.wait_ge(s_bv, s.count(WKV_LAG, 1))
                        nc.scalar.copy(kv[:, 1, m, :], ps[:, KVR_BANK + m, :]).then_inc(s_kv, 1)
                    act.wait_ge(s_rel, s.count(WKV_LAG, 1, 1))
                    for m in range(M):
                        nc.scalar.activation(ex[:, STATE_Y, m, :], rel[:, m, :], ACT.Relu, scale=-1.0,
                                             bias=vecs[:, FIRST + m:FIRST + m + 1]).then_inc(s_relu, 1)
                        nc.scalar.activation(ex[:, TOKEN_Y, m, :], rel[:, m, :], ACT.Relu,
                                             bias=neg_first[:, m:m + 1]).then_inc(s_relu, 1)
                    for i, (kind, scale) in enumerate(((STATE_W, 1.0), (TOKEN_W, -1.0))):
                        act.wait_ge(s_arg, s.count(WKV_LAG, 2 * M, M * (i + 1)))
                        nc.scalar.activation(ex[:, kind, :, :], ex[:, kind, :, :], ACT.Exp,
                                             scale=scale).then_inc(s_ex, 1)
                    act.wait_ge(s_relu, s.count(WKV_LAG, 2 * M, 2 * M))
                    nc.scalar.activation(ex[:, 0:2, :, :], ex[:, 0:2, :, :], ACT.Exp, scale=-1.0).then_inc(s_ex, 1)
                if wkv or o:
                    nc.scalar.preload_act_table(ACT.Gelu)
                if wkv:
                    for m in range(M):
                        act.wait_ge(s_kvr, s.count(WKV_LAG, 6, 2 * M + m + 1))
                        act.wait_ge(s_numr, s.count(WKV_LAG, 1))
                        nc.scalar.activation(r_tanh[:, m, :], ps[:, KVR_BANK + m, :], ACT.Tanh,
                                             scale=0.5).then_inc(s_rt, 1)
                gelu1(s, 2)
                if o:
                    for h in range(2):
                        act.wait_ge(s_tp, s.count(OUT_LAG, 2, h + 1))
                        act.wait_ge(s_gate, s.count(OUT_LAG, 2))
                        nc.scalar.activation(o_tanh[:, 2 * h:2 * h + 2, :], tok[:, 2 * h:2 * h + 2, :], ACT.Tanh,
                                             scale=0.5).then_inc(s_ot, 1)
                gelu1(s, 1)
                gelu1(s, 0)
                for layer in (gelu2, gelu3, tanh_logit, coupling):
                    for c in (2, 1, 0):
                        layer(s, c)
            run_slots(act, slot_body)

        @block.vector
        def _(dve):
            V = nc.vector
            V.memset(eps[:, :], LN_EPS).then_inc(s_eps, 1)
            dve.wait_ge(s_vec, 16)
            V.tensor_scalar(neg_first[:, :], vecs[:, FIRST:FIRST + M], -1.0, None, ALU.mult).then_inc(s_const, 1)
            V.tensor_scalar(half_b4[:, :], vecs[:, CN_B4:CN_B4 + 1], 0.5, None, ALU.mult).then_inc(s_const, 1)
            V.tensor_scalar(half_g3[:, :], vecs[:, GC_B3:GC_B3 + 1], 0.5, None, ALU.mult).then_inc(s_const, 1)
            V.tensor_tensor(range_sign[:, :], vecs[:, RANGE:RANGE + 1], vecs[:, SIGN:SIGN + 1],
                            ALU.mult).then_inc(s_const, 1)
            V.tensor_scalar(base_sign[:, :], vecs[:, SIGN:SIGN + 1], BASE_COUPLING, None,
                            ALU.mult).then_inc(s_const, 1)
            dve.wait_ge(s_const, 4)
            V.tensor_scalar(beta[:, :], range_sign[:, :], 0.3, None, ALU.mult).then_inc(s_const, 1)
            dve.wait_ge(s_decay, 1)
            V.tensor_scalar(decay[:, :], decay_pos[:, :], -1.0, None, ALU.mult).then_inc(s_const, 1)

            def tile_stats(g):
                dve.wait_ge(s_x[g % XS], 16 * (g // XS + 1))
                for k in range(SUB):
                    V.bn_stats(stats[:, g % 2, k, :], x_stage[:, g % XS, k, :]).then_inc(s_stat, 1)
                for k in range(SUB):
                    dve.wait_ge(s_stat, SUB * g + k + 1)
                    V.bn_aggr(meanvar[:, g, k, :], stats[:, g % 2, k, :]).then_inc(s_mv, 1)

            def normalise(g):
                dve.wait_ge(s_std, g + 1)
                V.reciprocal(rstd[:, g, :], std[:, g, :]).then_inc(s_rstd, 1)
                dve.wait_ge(s_rstd, g + 1)
                V.scalar_tensor_tensor(out=shift[:, g, :], in0=meanvar[:, g, :, 0], scalar=-1.0,
                                       in1=rstd[:, g, :], op0=ALU.mult, op1=ALU.mult).then_inc(s_shift, 1)
                if g >= 2:
                    dve.wait_ge(s_xt, M * (g - 1))
                for k in range(SUB // 2):
                    V.tensor_scalar(xn_stage[:, g % 2, k, :], x_stage[:, g % XS, k, :], meanvar[:, g, k, 0:1],
                                    rstd[:, g, k:k + 1], ALU.subtract, ALU.mult).then_inc(s_xn_v, 1)

            tile_stats(0)
            for g in range(NT):
                if g + 1 < NT:
                    tile_stats(g + 1)
                normalise(g)

            dve.wait_ge(s_wt, 16 * 11)
            V.tensor_scalar(w_o[:, :, :], w_o[:, :, :], 0.25, None, ALU.mult).then_inc(s_const, 1)
            dve.wait_ge(s_xe, M * NT)
            V.tensor_reduce(ctx_sum[:, :], tile_sums[:, :, :], AX_X, ALU.add).then_inc(s_sum, 1)
            dve.wait_ge(s_sum, 1)
            V.tensor_scalar(ctx_mean[:, :], ctx_sum[:, :], 1.0 / T, None, ALU.mult).then_inc(s_mean, 1)
            dve.wait_ge(s_ga, 3)
            V.tensor_tensor(alpha[:, :], range_sign[:, :], g_tanh[:, :], ALU.mult).then_inc(s_alpha, 1)
            dve.wait_ge(s_alpha, 1)
            V.scalar_tensor_tensor(out=alpha[:, :], in0=alpha[:, :], scalar=0.7, in1=base_sign[:, :],
                                   op0=ALU.mult, op1=ALU.add).then_inc(s_alpha, 1)

            def update(s, c):
                lag = c + 1
                if s.live(lag):
                    src = source(s, c, lag)
                    dve.wait_ge(s_cs[c], s.count(lag, 1, 1))
                    if c:
                        dve.wait_ge(s_st[c - 1], s.count(lag, M, M))
                    if c == 0 and s.live(OUT_LAG):
                        dve.wait_ge(s_st[2], s.count(OUT_LAG, M, M))
                    tu = turned[c % 2]
                    V.tensor_tensor(tu[:, :, :], coup[c][:, :].unsqueeze(1).to_broadcast([P, M, TN]), src,
                                    ALU.mult).then_inc(s_mul[c], 1)
                    dve.wait_ge(s_mul[c], s.count(lag, 1, 1))
                    if c + 1 < CYCLES:
                        dve.wait_ge(s_h1[c + 1], s.count(lag, M))
                        if s.live(lag + 1):
                            dve.wait_ge(s_st[c + 1], s.count(lag + 1, M, M))
                    else:
                        dve.wait_ge(s_tp, s.count(lag, 2))
                    V.tensor_tensor(state[c][:, 0, :], src[:, 0, :], tu[:, 1, :], ALU.add).then_inc(s_st[c], 1)
                    V.tensor_tensor(state[c][:, 1, :], src[:, 1, :], tu[:, 0, :],
                                    ALU.subtract).then_inc(s_st[c], 1)

            O, PN, Q = 0, 1, 2

            def slot_body(s):
                wkv, o = s.live(WKV_LAG), s.live(OUT_LAG)
                update(s, 2)
                update(s, 1)
                if wkv:
                    for m in range(M):
                        dve.wait_ge(s_kv, s.count(WKV_LAG, 2 * M, m + 1))
                        dve.wait_ge(s_carry, s.count(WKV_LAG, 1))
                        V.tensor_tensor_scan(opq[:, O, m, 1:1 + TN], decay[:, m:m + 1].to_broadcast([P, TN]),
                                             kv[:, 0, m, :], opq[:, O, m, 0:1], ALU.add, ALU.max).then_inc(s_o, 1)
                if o:
                    dve.wait_ge(s_rec, s.count(OUT_LAG, 1, 1))
                    dve.wait_ge(s_numr, s.count(OUT_LAG, 1, 1))
                    dve.wait_ge(s_proj, s.count(OUT_LAG, 2))
                    V.tensor_tensor(y[:, :, :], num[:, :, :], rec[:, :, :], ALU.mult).then_inc(s_y, 1)
                if wkv:
                    dve.wait_ge(s_o, s.count(WKV_LAG, M, M))
                    dve.wait_ge(s_relu, s.count(WKV_LAG, 2 * M))
                    V.tensor_tensor(rel[:, :, :], opq[:, O, :, 0:TN], kv[:, 0, :, :],
                                    ALU.subtract).then_inc(s_rel, 1)
                update(s, 0)
                if wkv:
                    dve.wait_ge(s_rel, s.count(WKV_LAG, 1, 1))
                    for kind, op in ((STATE_W, ALU.min), (TOKEN_W, ALU.max)):
                        for m in range(M):
                            V.tensor_scalar(ex[:, kind, m, :], rel[:, m, :], decay[:, m:m + 1], 0.0, ALU.add,
                                            op).then_inc(s_arg, 1)
                if s.live(1):
                    prev = xt_cols(s, 1, 0)
                    dve.wait_ge(s_diff, s.count(1, 1, 1))
                    dve.wait_ge(s_kvr, s.count(1, 6))
                    for w in range(3):
                        for m in range(M):
                            V.scalar_tensor_tensor(out=mixed[:, w, m, :], in0=diff[:, m, :],
                                                   scalar=vecs[:, MIX + M * w + m:MIX + M * w + m + 1],
                                                   in1=prev[:, m, :], op0=ALU.mult, op1=ALU.add
                                                   ).then_inc(s_mix, 1)
                if wkv:
                    dve.wait_ge(s_ex, s.count(WKV_LAG, 3, 2))
                    dve.wait_ge(s_kv, s.count(WKV_LAG, 2 * M, 2 * M))
                    V.tensor_tensor(b2v[:, :, :], ex[:, TOKEN_W, :, :], kv[:, 1, :, :], ALU.mult).then_inc(s_b2v, 1)
                    for m in range(M):
                        V.tensor_tensor_scan(opq[:, Q, m, 1:1 + TN], ex[:, STATE_W, m, :], ex[:, TOKEN_W, m, :],
                                             opq[:, Q, m, 0:1], ALU.mult, ALU.add).then_inc(s_q, 1)
                    dve.wait_ge(s_b2v, s.count(WKV_LAG, 1, 1))
                    for m in range(M):
                        V.tensor_tensor_scan(opq[:, PN, m, 1:1 + TN], ex[:, STATE_W, m, :], b2v[:, m, :],
                                             opq[:, PN, m, 0:1], ALU.mult, ALU.add).then_inc(s_p, 1)
                if o:
                    for h in range(2):
                        dve.wait_ge(s_ot, s.count(OUT_LAG, 2, h + 1))
                        V.scalar_tensor_tensor(out=gate[:, 2 * h:2 * h + 2, :], in0=o_tanh[:, 2 * h:2 * h + 2, :],
                                               scalar=1.0, in1=tok[:, 2 * h:2 * h + 2, :], op0=ALU.add,
                                               op1=ALU.mult).then_inc(s_gate, 1)
                if wkv:
                    dve.wait_ge(s_ex, s.count(WKV_LAG, 3, 3))
                    dve.wait_ge(s_q, s.count(WKV_LAG, M, M))
                    V.tensor_tensor(aq[:, :, :], ex[:, STATE_Y, :, :], opq[:, Q, :, 0:TN],
                                    ALU.mult).then_inc(s_aq, 1)
                    dve.wait_ge(s_p, s.count(WKV_LAG, M, M))
                    V.tensor_tensor(ap_[:, :, :], ex[:, STATE_Y, :, :], opq[:, PN, :, 0:TN],
                                    ALU.mult).then_inc(s_ap, 1)
                    dve.wait_ge(s_aq, s.count(WKV_LAG, 1, 1))
                    dve.wait_ge(s_ln, s.count(WKV_LAG, 1))
                    V.tensor_tensor(den[:, :, :], ex[:, TOKEN_Y, :, :], aq[:, :, :], ALU.add).then_inc(s_den, 1)
                    V.tensor_tensor(b2v[:, :, :], ex[:, TOKEN_Y, :, :], kv[:, 1, :, :], ALU.mult).then_inc(s_bv, 1)
                    dve.wait_ge(s_ap, s.count(WKV_LAG, 1, 1))
                    V.tensor_copy(opq[:, :, :, 0:1], opq[:, :, :, TN:TN + 1]).then_inc(s_carry, 1)
                    dve.wait_ge(s_bv, s.count(WKV_LAG, 1, 1))
                    V.tensor_tensor(num[:, :, :], ap_[:, :, :], b2v[:, :, :], ALU.add).then_inc(s_num, 1)
                    dve.wait_ge(s_num, s.count(WKV_LAG, 1, 1))
                    dve.wait_ge(s_rt, s.count(WKV_LAG, M, M))
                    V.scalar_tensor_tensor(out=num[:, :, :], in0=r_tanh[:, :, :], scalar=1.0, in1=num[:, :, :],
                                           op0=ALU.add, op1=ALU.mult).then_inc(s_numr, 1)
                if o:
                    dve.wait_ge(s_add, s.count(OUT_LAG, 1))
                    for h in range(2):
                        dve.wait_ge(s_proj, s.count(OUT_LAG, 2, h + 1))
                        V.tensor_tensor(gated[:, 2 * h:2 * h + 2, :], tok[:, 2 * h:2 * h + 2, :],
                                        gate[:, 2 * h:2 * h + 2, :], ALU.mult).then_inc(s_z, 1)
            run_slots(dve, slot_body)

        @block.tensor
        def _(pe):
            mm = nc.tensor.matmul
            pe.wait_ge(s_ident, 1)
            for g in range(NT):
                pe.wait_ge(s_xn_v, 2 * (g + 1))
                pe.wait_ge(s_xn_s, 2 * (g + 1))
                if g >= 4:
                    pe.wait_ge(s_xe, M * (g - 3))
                for m in range(M):
                    for k in range(SUB):
                        last = nc.tensor.transpose(ps[:, 2 * (g % 4) + m, k * P:(k + 1) * P],
                                                   xn_stage[:, g % 2, k, m * P:(m + 1) * P], ident[:, :])
                    last.then_inc(s_xt, 1)
            pe.wait_ge(s_wt, 16 * 11)
            pe.wait_ge(s_const, 8)
            pe.wait_ge(s_mean, 1)
            for m in range(M):
                last = mm(ps[:, KVR_BANK, 0:1], w_g1[:, m, :], ctx_mean[:, m:m + 1], start=(m == 0), stop=(m == 1))
            last.then_inc(s_gp, 1)
            pe.wait_ge(s_ga, 1)
            mm(ps[0:D3, KVR_BANK, 1:2], w_g2[:, :], g_h1[:, :], start=True, stop=True).then_inc(s_gp, 1)
            pe.wait_ge(s_ga, 2)
            mm(ps[:, KVR_BANK, 2:3], w_g3[0:D3, :], g_h2[0:D3, :], start=True, stop=True).then_inc(s_gp, 1)

            def project_kvr(s):
                if s.live(WKV_LAG):
                    for w in range(3):
                        pe.wait_ge(s_mix, s.count(WKV_LAG, 3 * M, M * (w + 1)))
                        for m in range(M):
                            if w == 0:
                                pe.wait_ge(s_z, s.count(OUT_LAG, 2))
                            else:
                                pe.wait_ge(s_kv, s.count(WKV_LAG, 2 * M, M * (w - 1) + m + 1))
                            for k in range(M):
                                last = mm(ps[:, KVR_BANK + m, :], w_kvr[:, w, k, m * P:(m + 1) * P],
                                          mixed[:, w, k, :], start=(k == 0), stop=(k == M - 1))
                            last.then_inc(s_kvr, 1)

            def layer1(s, c):
                if s.live(c):
                    src = source(s, c, c)
                    if c:
                        pe.wait_ge(s_st[c - 1], s.count(c, M, M))
                    pe.wait_ge(s_th[c], s.count(c, 1))
                    for m in range(M):
                        for k in range(M):
                            last = mm(ps[:, 2 * c + m, :], w_c1[:, k, m * P:(m + 1) * P], src[:, k, :],
                                      start=(k == 0), stop=(k == M - 1))
                        last.then_inc(s_h1[c], 1)

            def layer2(s, c):
                if s.live(c):
                    for k in range(M):
                        pe.wait_ge(s_g1[c], s.count(c, M, M))
                        last = mm(ps[:, 2 * c, :], w_c2[:, k, :], h1[c][:, k, :], start=(k == 0), stop=(k == M - 1))
                    last.then_inc(s_h2[c], 1)

            def layer3(s, c):
                if s.live(c):
                    pe.wait_ge(s_g2[c], s.count(c, 1, 1))
                    mm(ps[0:D3, 2 * c + 1, :], w_c3[:, :], h2[c][:, :], start=True, stop=True).then_inc(s_h3[c], 1)

            def logits(s, c):
                if s.live(c):
                    pe.wait_ge(s_g3[c], s.count(c, 1, 1))
                    mm(ps[:, 2 * c, :], w_c4[0:D3, :], h3[c][0:D3, :], start=True, stop=True).then_inc(s_lg[c], 1)

            def slot_body(s):
                o = s.live(OUT_LAG)
                project_kvr(s)
                layer1(s, 2)
                if o:
                    pe.wait_ge(s_st[2], s.count(OUT_LAG, M, M))
                    for h in range(2):
                        pe.wait_ge(s_rt, s.count(WKV_LAG, M, h + 1))
                        pe.wait_ge(s_z, s.count(OUT_LAG, 2))
                        for k in (2 * h, 2 * h + 1):
                            for m in range(M):
                                last = nc.tensor.transpose(tok[:, k, m * P:(m + 1) * P],
                                                           state[2][:, m, k * P:(k + 1) * P], ident[:, :])
                        last.then_inc(s_tp, 1)
                layer1(s, 1)
                layer1(s, 0)
                for c in (2, 1, 0):
                    layer2(s, c)
                if o:
                    pe.wait_ge(s_y, s.count(OUT_LAG, 1, 1))
                    for h in range(2):
                        pe.wait_ge(s_gate, s.count(OUT_LAG, 2, h + 1))
                        for k in (2 * h, 2 * h + 1):
                            for m in range(M):
                                last = mm(tok[:, k, :], y[:, m, k * P:(k + 1) * P], w_o[:, m, :],
                                          start=(m == 0), stop=(m == M - 1))
                        last.then_inc(s_proj, 1)
                for c in (2, 1, 0):
                    layer3(s, c)
                for c in (2, 1, 0):
                    logits(s, c)
            run_slots(pe, slot_body)


def kernel(**inputs):
    import numpy as np
    import concourse.bacc as bacc
    from concourse import mybir as _mybir
    from concourse.bass_utils import run_bass_kernel_spmd as run

    a = {k: np.asarray(v) for k, v in inputs.items()}
    x = a["L0_attn_x"]
    T, C = x.shape[1:]

    def chunks(v):
        return np.ascontiguousarray(v.reshape(-1, P).T)

    vec = np.zeros((P, NVEC), np.float32)
    vec[:, DECAY:DECAY + 2] = chunks(a["L0_attn_time_decay"])
    vec[:, FIRST:FIRST + 2] = chunks(a["L0_attn_time_first"])
    for i, n in enumerate("kvr"):
        vec[:, MIX + 2 * i:MIX + 2 * i + 2] = chunks(a[f"L0_attn_time_mix_{n}"])
    vec[:, CN_B1:CN_B1 + 2] = chunks(a["L0_ffn_cn_b1"])
    vec[:, CN_B2] = a["L0_ffn_cn_b2"]
    vec[0:64, CN_B3] = a["L0_ffn_cn_b3"]
    vec[:, CN_B4] = a["L0_ffn_cn_b4"]
    vec[:, GC_B1] = a["L0_ffn_gc_b1"]
    vec[0:64, GC_B2] = a["L0_ffn_gc_b2"]
    vec[:, GC_B3] = a["L0_ffn_gc_b3"]
    vec[:, RANGE] = a["L0_ffn_adaptive_range"]
    vec[0:64, SIGN] = 1.0
    vec[64:P, SIGN] = -1.0

    arrays = {
        "x": x.reshape(T, C), "vec": vec,
        "wk_t": a["L0_attn_Wk"].T, "wv_t": a["L0_attn_Wv"].T, "wr_t": a["L0_attn_Wr"].T, "wo_t": a["L0_attn_Wo"].T,
        "cn_w1": a["L0_ffn_cn_w1"], "cn_w2": a["L0_ffn_cn_w2"], "cn_w3": a["L0_ffn_cn_w3"],
        "cn_w4": np.repeat(a["L0_ffn_cn_w4"], P, axis=1),
        "gc_w1": a["L0_ffn_gc_w1"], "gc_w2": a["L0_ffn_gc_w2"],
        "gc_w3": np.repeat(a["L0_ffn_gc_w3"], P, axis=1),
    }
    arrays = {k: np.ascontiguousarray(v) for k, v in arrays.items()}
    nc = bacc.Bacc("TRN2", target_bir_lowering=False, num_devices=1)
    args = [nc.dram_tensor(k, v.shape, _mybir.dt.from_np(v.dtype), kind="ExternalInput").ap()
            for k, v in arrays.items()]
    out = nc.dram_tensor("out", (T, C), F32, kind="ExternalOutput").ap()
    rwkv_coupled_ffn(nc, *args, out)
    r = run(nc, [arrays], core_ids=[0])
    return r.results[0]["out"].reshape(1, T, C)
```

```python
from contextlib import ExitStack

import concourse.bass as bass
from concourse import mybir

F32 = mybir.dt.float32
ALU = mybir.AluOpType
ACT = mybir.ActivationFunctionType
AX_X = mybir.AxisListType.X

P = 128
EXP_LN_SET = "natural_log_exp_and_others"
LN_EPS = 1e-5
NEG_INF = -1e38
BASE_COUPLING = 0.1
CYCLES = 3
AHEAD = CYCLES
NET_LAG = (-AHEAD, 0, 1)
WKV_LAG = 1
OUT_LAG = 2

DECAY, FIRST, MIX, CN_B1, CN_B2, CN_B3, CN_B4, GC_B1, GC_B2, GC_B3, RANGE, SIGN, NVEC = (
    0, 2, 4, 10, 12, 13, 14, 15, 16, 17, 18, 19, 20)


class Slot:

    def __init__(self, tiles, base, reg=None):
        self.tiles, self.base, self.reg = tiles, base, reg

    def live(self, lag):
        return 0 <= self.base - lag < self.tiles

    def count(self, lag, per_tile, k=0):
        const = per_tile * (self.base - lag) + k
        if self.reg is None:
            return max(0, min(const, per_tile * self.tiles))
        assert const > 0
        return self.reg * per_tile + const

    def round(self, chain, per_round, k=0):
        const = per_round * (self.base - max(NET_LAG[chain], 0) + 1) + k
        return const if self.reg is None else self.reg * per_round + const

    def tile(self, lag):
        return self.base - lag if self.reg is None else self.reg + (self.base - lag)


def rwkv_coupled_ffn(nc, x, vec, wk_t, wv_t, wr_t, wo_t, cn_w1, cn_w2, cn_w3, cn_w4, gc_w1, gc_w2, gc_w3, out):
    T, C = x.shape
    M = C // P
    TN = 512
    NT = T // TN
    SUB = TN // P
    D2 = cn_w2.shape[1]
    D3 = cn_w3.shape[1]
    SLOTS = NT + OUT_LAG
    LOOPS = ((OUT_LAG + 1, NT - AHEAD), (NT - AHEAD, NT))
    assert M == 2 and D2 == P and D3 == 64 and SUB * C == 2 * TN

    x_tiles = x.rearrange("(g s p) c -> g p s c", s=SUB, p=P)
    out_tiles = out.rearrange("(g s p) c -> g p s c", s=SUB, p=P)

    with ExitStack() as ctx:
        def sb(name, *shape):
            return ctx.enter_context(nc.sbuf_tensor(name, [P, *shape], F32))

        def sem(name):
            return ctx.enter_context(nc.semaphore(name))

        vecs = sb("vecs", NVEC)
        w_kvr = sb("w_kvr", 3, M, C)
        w_o = sb("w_o", M, C)
        w_c1 = sb("w_c1", M, C)
        w_c2 = sb("w_c2", M, D2)
        w_c3 = sb("w_c3", D3)
        w_c4 = sb("w_c4", P)
        w_g1 = sb("w_g1", M, D2)
        w_g2 = sb("w_g2", D3)
        w_g3 = sb("w_g3", P)
        ident = sb("ident", P)
        decay_pos = sb("decay_pos", M)
        decay = sb("decay", M)
        neg_first = sb("neg_first", M)
        half_b4 = sb("half_b4", 1)
        half_g3 = sb("half_g3", 1)
        beta = sb("beta", 1)
        alpha = sb("alpha", 1)
        range_sign = sb("range_sign", 1)
        base_sign = sb("base_sign", 1)
        stats = sb("stats", NT, SUB, 6)
        meanvar = sb("meanvar", NT, SUB, 2)
        var_eps = sb("var_eps", NT, SUB)
        power = sb("power", SUB)
        rstd = sb("rstd", NT, SUB)
        shift = sb("shift", NT, SUB)
        tile_sums = sb("tile_sums", M, NT)
        ctx_sum = sb("ctx_sum", M)
        ctx_mean = sb("ctx_mean", M)
        g_h1 = sb("g_h1", 1)
        g_h2 = sb("g_h2", 1)
        g_tanh = sb("g_tanh", 1)
        xt = sb("xt", M, 1 + T)
        diff = sb("diff", M, TN)
        mixed = sb("mixed", 3, M, TN)
        kv = sb("kv", 2, M, TN)
        r_tanh = sb("r_tanh", M, TN)
        rel = sb("rel", M, TN)
        ex = sb("ex", 4, M, TN)
        STATE_Y, TOKEN_Y, STATE_W, TOKEN_W = range(4)
        opq = sb("opq", 3, M, 1 + TN)
        b2v = sb("b2v", M, TN)
        den = sb("den", M, TN)
        num = sb("num", M, TN)
        rec = sb("rec", M, TN)
        y = sb("y", M, TN)
        h1 = [sb(f"h1_{c}", M, TN) for c in range(CYCLES)]
        h2 = [sb(f"h2_{c}", TN) for c in range(CYCLES)]
        h3 = [sb(f"h3_{c}", TN) for c in range(CYCLES)]
        tanh_0 = sb("tanh_0", NT, TN)
        tanh_c = [None] + [sb(f"tanh_{c}", TN) for c in range(1, CYCLES)]
        coup = [sb(f"coup_{c}", TN) for c in range(CYCLES)]
        turned = [b2v, sb("turned", M, TN)]
        state = [sb(f"state_{c}", M, TN) for c in range(CYCLES)]
        o_tanh = sb("o_tanh", SUB, C)
        gate = sb("gate", SUB, C)
        resid = sb("resid", SUB, C)
        XS = 4
        x_stage = ex[:, :, :, :].rearrange("p a m t -> p a (m t)").rearrange("p a (s c) -> p a s c", c=C)
        xn_stage = kv[:, :, :, :].rearrange("p a m t -> p a (m t)").rearrange("p a (s c) -> p a s c", c=C)

        ps = ctx.enter_context(nc.psum_tensor("ps", [P, 8, TN], F32))
        KVR_BANK = 2 * CYCLES
        tok = ps[:, KVR_BANK:KVR_BANK + 2, :].rearrange("p b t -> p (b t)").rearrange("p (s c) -> p s c", c=C)

        s_vec = sem("vec_loaded")
        s_wc = sem("coupling_weights_loaded")
        s_wg = sem("global_weights_loaded")
        s_wt = sem("rwkv_weights_loaded")
        s_x = [sem(f"x_loaded_{i}") for i in range(XS)]
        s_zero = sem("ident_zeroed")
        s_ident = sem("ident_ready")
        s_init = sem("carries_ready")
        s_decay = sem("decay_ready")
        s_const = sem("constants_ready")
        s_power = sem("power_ready")
        s_stat = sem("stats_done")
        s_mv = sem("meanvar_done")
        s_ve = sem("variance_plus_eps_done")
        s_rstd = sem("rstd_done")
        s_shift = sem("shift_done")
        s_xn_v = sem("xn_vector_done")
        s_xn_s = sem("xn_scalar_done")
        s_xn_p = sem("xn_pool_done")
        s_xt = sem("xt_transposed")
        s_xe = sem("xt_stored")
        s_sum = sem("context_summed")
        s_mean = sem("context_mean_done")
        s_gp = sem("global_layer_done")
        s_ga = sem("global_act_done")
        s_alpha = sem("alpha_ready")
        s_diff = sem("diff_done")
        s_mix = sem("mix_done")
        s_kvr = sem("kvr_done")
        s_kv = sem("kv_stored")
        s_r = sem("r_stored")
        s_rt = sem("r_tanh_done")
        s_o = sem("o_scanned")
        s_rel = sem("rel_done")
        s_relu = sem("output_exponents_done")
        s_arg = sem("state_exponents_done")
        s_ex = sem("exps_done")
        s_b2v = sem("b2v_done")
        s_q = sem("q_scanned")
        s_p = sem("p_scanned")
        s_aq = sem("aq_done")
        s_ap = sem("ap_done")
        s_den = sem("den_done")
        s_bv = sem("bv_done")
        s_num = sem("num_done")
        s_numr = sem("num_times_r_done")
        s_carry = sem("carry_done")
        s_ln = sem("ln_done")
        s_rec = sem("rec_done")
        s_y = sem("y_done")
        s_h1 = [sem(f"h1_pre_{c}") for c in range(CYCLES)]
        s_h2 = [sem(f"h2_pre_{c}") for c in range(CYCLES)]
        s_h3 = [sem(f"h3_pre_{c}") for c in range(CYCLES)]
        s_lg = [sem(f"logit_{c}") for c in range(CYCLES)]
        s_g1 = [sem(f"h1_done_{c}") for c in range(CYCLES)]
        s_g2 = [sem(f"h2_done_{c}") for c in range(CYCLES)]
        s_g3 = [sem(f"h3_done_{c}") for c in range(CYCLES)]
        s_th = [sem(f"tanh_done_{c}") for c in range(CYCLES)]
        s_cs = [sem(f"coupling_done_{c}") for c in range(CYCLES)]
        s_mul = [sem(f"turn_done_{c}") for c in range(CYCLES)]
        s_st = [sem(f"state_done_{c}") for c in range(CYCLES)]
        s_tp = sem("out_transposed")
        s_ot = sem("o_tanh_done")
        s_gate = sem("gate_done")
        s_proj = sem("out_projected")
        s_z = sem("gated_done")
        s_xr = sem("residual_loaded")
        s_add = sem("sum_done")
        s_out = sem("out_stored")

        def run_slots(eng, slot_body):
            for j in range(LOOPS[0][0]):
                slot_body(Slot(NT, j))
            for first, end in LOOPS:
                with eng.Fori(0, end - first) as i:
                    slot_body(Slot(NT, first, i))
            for j in range(LOOPS[-1][1], SLOTS):
                slot_body(Slot(NT, j))

        def xt_cols(slot, lag, first=1):
            if slot.reg is None:
                at = (slot.base - lag) * TN + first
                return xt[:, :, at:at + TN]
            return xt[:, :, bass.ds(slot.reg * TN + ((slot.base - lag) * TN + first), TN)]

        def prologue_cols(t):
            return xt[:, :, 1 + t * TN:1 + (t + 1) * TN]

        def source(slot, cycle, lag):
            return xt_cols(slot, lag) if cycle == 0 else state[cycle - 1][:, :, :]

        PROLOGUE_NET = {1: [(0, 0)], 2: [(0, 1)], 3: [(0, 2)], 4: [(1, 0)], 5: [(1, 1)], 6: [(1, 2)],
                        7: [(2, 0), (2, 1), (2, 2)]}

        block = ctx.enter_context(nc.Block())

        @block.sync
        def _(sp):
            def rows(w):
                return w.rearrange("(k p) n -> p k n", p=P)

            def load_x(g):
                if g >= XS:
                    sp.wait_ge(s_xn_v, g - XS + 1)
                    sp.wait_ge(s_xn_s, 2 * (g - XS + 1))
                    sp.wait_ge(s_xn_p, g - XS + 1)
                sp.dma_start(x_stage[:, g % XS, :, :], x_tiles[g]).then_inc(s_x[g % XS], 16)

            def load_w(dst, src, loaded):
                sp.dma_start(dst, src).then_inc(loaded, 16)

            load_x(0)
            sp.dma_start(vecs[:, :], vec).then_inc(s_vec, 16)
            load_x(1)
            load_w(w_c1[:, :, :], rows(cn_w1), s_wc)
            load_x(2)
            load_w(w_c2[:, :, :], rows(cn_w2), s_wc)
            load_x(3)
            load_w(w_c3[:, :], cn_w3, s_wc)
            load_w(w_c4[0:D3, :], cn_w4, s_wc)
            load_x(4)
            load_w(w_g1[:, :, :], rows(gc_w1), s_wg)
            load_w(w_g2[:, :], gc_w2, s_wg)
            load_w(w_g3[0:D3, :], gc_w3, s_wg)
            load_x(5)
            for i, w in enumerate((wk_t, wv_t, wr_t)):
                load_w(w_kvr[:, i, :, :], rows(w), s_wt)
            load_x(6)
            load_w(w_o[:, :, :], rows(wo_t), s_wt)
            load_x(7)

            def slot_body(s):
                if s.live(OUT_LAG):
                    sp.wait_ge(s_out, s.count(OUT_LAG, 16))
                    sp.dma_start(resid[:, :, :], x_tiles[s.tile(OUT_LAG)]).then_inc(s_xr, 16)
                    sp.wait_ge(s_add, s.count(OUT_LAG, 1, 1))
                    sp.dma_start(out_tiles[s.tile(OUT_LAG)], resid[:, :, :]).then_inc(s_out, 16)
            run_slots(sp, slot_body)
            sp.wait_ge(s_out, 16 * NT)

        @block.gpsimd
        def _(pool):
            nc.gpsimd.memset(ident[:, :], 0.0).then_inc(s_zero, 1)
            pool.wait_ge(s_zero, 1)
            nc.gpsimd.affine_select(out=ident[:, :], in_=ident[:, :], compare_op=ALU.not_equal, fill=1.0,
                                    base=0, pattern=[[-1, P]], channel_multiplier=1).then_inc(s_ident, 1)
            nc.gpsimd.memset(xt[:, :, 0:1], 0.0).then_inc(s_init, 1)
            nc.gpsimd.memset(opq[:, 0, :, 0:1], NEG_INF).then_inc(s_init, 1)
            nc.gpsimd.memset(opq[:, 1:3, :, 0:1], 0.0).then_inc(s_init, 1)
            pool.wait_ge(s_init, 3)
            nc.gpsimd.memset(power[:, :], -0.5).then_inc(s_power, 1)
            pool.wait_ge(s_power, 1)

            def inverse_std(g):
                pool.wait_ge(s_mv, SUB * (g + 1))
                nc.gpsimd.tensor_scalar(var_eps[:, g, :], meanvar[:, g, :, 1], 1.0, LN_EPS, ALU.mult,
                                        ALU.add).then_inc(s_ve, 1)
                pool.wait_ge(s_ve, g + 1)
                nc.gpsimd.tensor_tensor(rstd[:, g, :], var_eps[:, g, :], power[:, :], ALU.pow).then_inc(s_rstd, 1)

            inverse_std(0)
            for g in range(NT):
                if g + 1 < NT:
                    inverse_std(g + 1)
                pool.wait_ge(s_shift, g + 1)
                if g >= 2:
                    pool.wait_ge(s_xt, M * (g - 1))
                nc.gpsimd.tensor_scalar(xn_stage[:, g % 2, 1, :], x_stage[:, g % XS, 1, :], rstd[:, g, 1:2],
                                        shift[:, g, 1:2], ALU.mult, ALU.add).then_inc(s_xn_p, 1)
            pool.wait_ge(s_xe, M * NT)

            def slot_body(s):
                if s.live(0):
                    pool.wait_ge(s_mix, s.count(0, 3 * M))
                    nc.gpsimd.tensor_tensor(diff[:, :, :], xt_cols(s, 0), xt_cols(s, 0, 0),
                                            ALU.subtract).then_inc(s_diff, 1)
                if s.live(OUT_LAG):
                    pool.wait_ge(s_xr, s.count(OUT_LAG, 16, 16))
                    pool.wait_ge(s_z, s.count(OUT_LAG, 2, 2))
                    nc.gpsimd.tensor_tensor(resid[:, :, :], gate[:, :, :], resid[:, :, :],
                                            ALU.add).then_inc(s_add, 1)
            run_slots(pool, slot_body)

        @block.scalar
        def _(act):
            act.wait_ge(s_vec, 16)
            nc.scalar.activation(decay_pos[:, :], vecs[:, DECAY:DECAY + M], ACT.Exp).then_inc(s_decay, 1)
            act.wait_ge(s_const, 7)

            def gelu1(c, round_start):
                for m in range(M):
                    act.wait_ge(s_h1[c], round_start(c, M, m + 1))
                    nc.scalar.activation(h1[c][:, m, :], ps[:, 2 * c + m, :], ACT.Gelu,
                                         bias=vecs[:, CN_B1 + m:CN_B1 + m + 1]).then_inc(s_g1[c], 1)

            def gelu2(c, round_start):
                act.wait_ge(s_h2[c], round_start(c, 1, 1))
                nc.scalar.activation(h2[c][:, :], ps[:, 2 * c, :], ACT.Gelu,
                                     bias=vecs[:, CN_B2:CN_B2 + 1]).then_inc(s_g2[c], 1)

            def gelu3(c, round_start):
                act.wait_ge(s_h3[c], round_start(c, 1, 1))
                nc.scalar.activation(h3[c][0:D3, :], ps[0:D3, 2 * c + 1, :], ACT.Gelu,
                                     bias=vecs[0:D3, CN_B3:CN_B3 + 1]).then_inc(s_g3[c], 1)

            def tanh_logit(c, round_start, dst):
                act.wait_ge(s_lg[c], round_start(c, 1, 1))
                nc.scalar.activation(dst, ps[:, 2 * c, :], ACT.Tanh, scale=0.5,
                                     bias=half_b4[:, :]).then_inc(s_th[c], 1)

            def prologue_round(c, per_round, k):
                return k

            def normalise(g):
                act.wait_ge(s_shift, g + 1)
                if g >= 2:
                    act.wait_ge(s_xt, M * (g - 1))
                for k in range(SUB // 2, SUB):
                    nc.scalar.activation(xn_stage[:, g % 2, k, :], x_stage[:, g % XS, k, :], ACT.Identity,
                                         bias=shift[:, g, k:k + 1], scale=rstd[:, g, k:k + 1]
                                         ).then_inc(s_xn_s, 1)

            def store_xt(g):
                for m in range(M):
                    act.wait_ge(s_xt, M * g + m + 1)
                    nc.scalar.activation(xt[:, m, 1 + g * TN:1 + (g + 1) * TN], ps[:, KVR_BANK + m, :],
                                         ACT.Identity, accum_out=tile_sums[:, m, g:g + 1]).then_inc(s_xe, 1)

            nc.scalar.preload_act_table(ACT.Gelu)
            normalise(0)
            for g in range(NT):
                if g + 1 < NT:
                    normalise(g + 1)
                store_xt(g)
                for layer, t in PROLOGUE_NET.get(g, ()):
                    (gelu1, gelu2, gelu3)[layer](t, prologue_round)
            act.wait_ge(s_gp, 1)
            nc.scalar.activation(g_h1[:, :], ps[:, KVR_BANK, 0:1], ACT.Gelu,
                                 bias=vecs[:, GC_B1:GC_B1 + 1]).then_inc(s_ga, 1)
            tanh_logit(0, prologue_round, tanh_0[:, 0, :])
            act.wait_ge(s_gp, 2)
            nc.scalar.activation(g_h2[0:D3, :], ps[0:D3, KVR_BANK, 1:2], ACT.Gelu,
                                 bias=vecs[0:D3, GC_B2:GC_B2 + 1]).then_inc(s_ga, 1)
            tanh_logit(1, prologue_round, tanh_0[:, 1, :])
            act.wait_ge(s_gp, 3)
            nc.scalar.activation(g_tanh[:, :], ps[:, KVR_BANK, 2:3], ACT.Tanh, scale=0.5,
                                 bias=half_g3[:, :]).then_inc(s_ga, 1)
            tanh_logit(2, prologue_round, tanh_0[:, 2, :])
            act.wait_ge(s_alpha, 2)
            for c in range(1, CYCLES):
                act.wait_ge(s_th[c], 1)

            def coupling(s, c):
                lag = max(NET_LAG[c], 0)
                if s.live(lag):
                    if c == 0:
                        act.wait_ge(s_th[0], max(1, s.base - AHEAD + 2) + (0 if s.reg is None else s.reg))
                        th = tanh_0[:, s.tile(0), :] if s.reg is None else tanh_0[
                            :, :, :].rearrange("p g t -> p (g t)")[:, bass.ds(s.reg * TN + s.base * TN, TN)]
                    else:
                        act.wait_ge(s_th[c], s.round(c, 1, 1))
                        th = tanh_c[c][:, :]
                    act.wait_ge(s_mul[c], s.count(lag, 1))
                    nc.scalar.activation(coup[c][:, :], th, ACT.Identity, scale=beta[:, :],
                                         bias=alpha[:, :]).then_inc(s_cs[c], 1)

            def slot_body(s):
                wkv, o = s.live(WKV_LAG), s.live(OUT_LAG)
                if wkv:
                    for m in range(M):
                        act.wait_ge(s_kvr, s.count(WKV_LAG, 6, m + 1))
                        act.wait_ge(s_rel, s.count(WKV_LAG, 1))
                        nc.scalar.copy(kv[:, 0, m, :], ps[:, KVR_BANK + m, :]).then_inc(s_kv, 1)
                coupling(s, 0)
                if wkv or o:
                    nc.scalar.preload_act_table_set(EXP_LN_SET)
                def store_v(m):
                    act.wait_ge(s_kvr, s.count(WKV_LAG, 6, M + m + 1))
                    act.wait_ge(s_bv, s.count(WKV_LAG, 1))
                    nc.scalar.copy(kv[:, 1, m, :], ps[:, KVR_BANK + m, :]).then_inc(s_kv, 1)

                if o:
                    act.wait_ge(s_den, s.count(OUT_LAG, 1, 1))
                    act.wait_ge(s_y, s.count(OUT_LAG, 1))
                    nc.scalar.activation(rec[:, :, :], den[:, :, :], ACT.Ln).then_inc(s_ln, 1)
                if wkv:
                    store_v(0)
                if o:
                    act.wait_ge(s_ln, s.count(OUT_LAG, 1, 1))
                    nc.scalar.activation(rec[:, :, :], rec[:, :, :], ACT.Exp, scale=-1.0).then_inc(s_rec, 1)
                if wkv:
                    store_v(1)
                    act.wait_ge(s_rel, s.count(WKV_LAG, 1, 1))
                    for m in range(M):
                        nc.scalar.activation(ex[:, STATE_Y, m, :], rel[:, m, :], ACT.Relu, scale=-1.0,
                                             bias=vecs[:, FIRST + m:FIRST + m + 1]).then_inc(s_relu, 1)
                        nc.scalar.activation(ex[:, TOKEN_Y, m, :], rel[:, m, :], ACT.Relu,
                                             bias=neg_first[:, m:m + 1]).then_inc(s_relu, 1)
                    for m in range(M):
                        act.wait_ge(s_kvr, s.count(WKV_LAG, 6, 2 * M + m + 1))
                        act.wait_ge(s_numr, s.count(WKV_LAG, 1))
                        nc.scalar.copy(r_tanh[:, m, :], ps[:, KVR_BANK + m, :]).then_inc(s_r, 1)
                    for i, (kind, scale) in enumerate(((STATE_W, 1.0), (TOKEN_W, -1.0))):
                        act.wait_ge(s_arg, s.count(WKV_LAG, 2 * M, M * (i + 1)))
                        nc.scalar.activation(ex[:, kind, :, :], ex[:, kind, :, :], ACT.Exp,
                                             scale=scale).then_inc(s_ex, 1)
                    act.wait_ge(s_relu, s.count(WKV_LAG, 2 * M, 2 * M))
                    nc.scalar.activation(ex[:, 0:2, :, :], ex[:, 0:2, :, :], ACT.Exp, scale=-1.0).then_inc(s_ex, 1)
                if wkv or o:
                    nc.scalar.preload_act_table(ACT.Gelu)
                if wkv:
                    act.wait_ge(s_r, s.count(WKV_LAG, M, M))
                    nc.scalar.activation(r_tanh[:, :, :], r_tanh[:, :, :], ACT.Tanh, scale=0.5).then_inc(s_rt, 1)
                nets = [c for c in (2, 1, 0) if s.live(NET_LAG[c])]
                for c in (2, 0):
                    if c in nets:
                        gelu1(c, s.round)
                if o:
                    for h in range(2):
                        act.wait_ge(s_tp, s.count(OUT_LAG, 2, h + 1))
                        act.wait_ge(s_gate, s.count(OUT_LAG, 2))
                        nc.scalar.activation(o_tanh[:, 2 * h:2 * h + 2, :], tok[:, 2 * h:2 * h + 2, :], ACT.Tanh,
                                             scale=0.5).then_inc(s_ot, 1)
                if 1 in nets:
                    gelu1(1, s.round)
                for layer in (gelu2, gelu3):
                    for c in nets:
                        layer(c, s.round)
                for c in nets:
                    if c:
                        tanh_logit(c, s.round, tanh_c[c][:, :])
                    elif s.reg is None:
                        tanh_logit(0, s.round, tanh_0[:, s.tile(NET_LAG[0]), :])
                    else:
                        tanh_logit(0, s.round, tanh_0[:, :, :].rearrange("p g t -> p (g t)")[
                            :, bass.ds(s.reg * TN + (s.base + AHEAD) * TN, TN)])
                for c in (2, 1):
                    coupling(s, c)
            run_slots(act, slot_body)

        @block.vector
        def _(dve):
            V = nc.vector
            dve.wait_ge(s_vec, 16)
            V.tensor_scalar(neg_first[:, :], vecs[:, FIRST:FIRST + M], -1.0, None, ALU.mult).then_inc(s_const, 1)
            V.tensor_scalar(half_b4[:, :], vecs[:, CN_B4:CN_B4 + 1], 0.5, None, ALU.mult).then_inc(s_const, 1)
            V.tensor_scalar(half_g3[:, :], vecs[:, GC_B3:GC_B3 + 1], 0.5, None, ALU.mult).then_inc(s_const, 1)
            V.tensor_tensor(range_sign[:, :], vecs[:, RANGE:RANGE + 1], vecs[:, SIGN:SIGN + 1],
                            ALU.mult).then_inc(s_const, 1)
            V.tensor_scalar(base_sign[:, :], vecs[:, SIGN:SIGN + 1], BASE_COUPLING, None,
                            ALU.mult).then_inc(s_const, 1)
            dve.wait_ge(s_const, 4)
            V.tensor_scalar(beta[:, :], range_sign[:, :], 0.3, None, ALU.mult).then_inc(s_const, 1)
            dve.wait_ge(s_decay, 1)
            V.tensor_scalar(decay[:, :], decay_pos[:, :], -1.0, None, ALU.mult).then_inc(s_const, 1)

            def tile_stats(g):
                dve.wait_ge(s_x[g % XS], 16 * (g // XS + 1))
                for k in range(SUB):
                    V.bn_stats(stats[:, g, k, :], x_stage[:, g % XS, k, :]).then_inc(s_stat, 1)
                for k in range(SUB):
                    dve.wait_ge(s_stat, SUB * g + k + 1)
                    V.bn_aggr(meanvar[:, g, k, :], stats[:, g, k, :]).then_inc(s_mv, 1)

            def tile_shift(g):
                dve.wait_ge(s_rstd, g + 1)
                V.scalar_tensor_tensor(out=shift[:, g, :], in0=meanvar[:, g, :, 0], scalar=-1.0,
                                       in1=rstd[:, g, :], op0=ALU.mult, op1=ALU.mult).then_inc(s_shift, 1)

            tile_stats(0)
            tile_stats(1)
            tile_shift(0)
            for g in range(NT):
                if g + 2 < NT:
                    tile_stats(g + 2)
                if g + 1 < NT:
                    tile_shift(g + 1)
                if g >= 2:
                    dve.wait_ge(s_xt, M * (g - 1))
                V.tensor_scalar(xn_stage[:, g % 2, 0, :], x_stage[:, g % XS, 0, :], meanvar[:, g, 0, 0:1],
                                rstd[:, g, 0:1], ALU.subtract, ALU.mult).then_inc(s_xn_v, 1)

            dve.wait_ge(s_wt, 16 * 4)
            V.tensor_scalar(w_o[:, :, :], w_o[:, :, :], 0.25, None, ALU.mult).then_inc(s_const, 1)
            dve.wait_ge(s_xe, M * NT)
            V.tensor_reduce(ctx_sum[:, :], tile_sums[:, :, :], AX_X, ALU.add).then_inc(s_sum, 1)
            dve.wait_ge(s_sum, 1)
            V.tensor_scalar(ctx_mean[:, :], ctx_sum[:, :], 1.0 / T, None, ALU.mult).then_inc(s_mean, 1)
            dve.wait_ge(s_ga, 3)
            V.tensor_tensor(alpha[:, :], range_sign[:, :], g_tanh[:, :], ALU.mult).then_inc(s_alpha, 1)
            dve.wait_ge(s_alpha, 1)
            V.scalar_tensor_tensor(out=alpha[:, :], in0=alpha[:, :], scalar=0.7, in1=base_sign[:, :],
                                   op0=ALU.mult, op1=ALU.add).then_inc(s_alpha, 1)

            def update(s, c):
                lag = c
                if s.live(lag):
                    src = source(s, c, lag)
                    dve.wait_ge(s_cs[c], s.count(lag, 1, 1))
                    if c:
                        dve.wait_ge(s_st[c - 1], s.count(lag, M, M))
                    if c == 0 and s.live(OUT_LAG):
                        dve.wait_ge(s_st[2], s.count(OUT_LAG, M, M))
                    tu = turned[c % 2]
                    V.tensor_tensor(tu[:, :, :], coup[c][:, :].unsqueeze(1).to_broadcast([P, M, TN]), src,
                                    ALU.mult).then_inc(s_mul[c], 1)
                    dve.wait_ge(s_mul[c], s.count(lag, 1, 1))
                    if c + 1 < CYCLES:
                        dve.wait_ge(s_h1[c + 1], s.count(lag, M, M))
                        if s.live(lag + 1):
                            dve.wait_ge(s_st[c + 1], s.count(lag + 1, M, M))
                    else:
                        dve.wait_ge(s_tp, s.count(lag, 2))
                    V.tensor_tensor(state[c][:, 0, :], src[:, 0, :], tu[:, 1, :], ALU.add).then_inc(s_st[c], 1)
                    V.tensor_tensor(state[c][:, 1, :], src[:, 1, :], tu[:, 0, :],
                                    ALU.subtract).then_inc(s_st[c], 1)

            O, PN, Q = 0, 1, 2

            def slot_body(s):
                wkv, o = s.live(WKV_LAG), s.live(OUT_LAG)
                update(s, 2)
                update(s, 1)
                if wkv:
                    for m in range(M):
                        dve.wait_ge(s_kv, s.count(WKV_LAG, 2 * M, m + 1))
                        dve.wait_ge(s_carry, s.count(WKV_LAG, 1))
                        V.tensor_tensor_scan(opq[:, O, m, 1:1 + TN], decay[:, m:m + 1].to_broadcast([P, TN]),
                                             kv[:, 0, m, :], opq[:, O, m, 0:1], ALU.add, ALU.max).then_inc(s_o, 1)
                if wkv:
                    dve.wait_ge(s_o, s.count(WKV_LAG, M, M))
                    dve.wait_ge(s_relu, s.count(WKV_LAG, 2 * M))
                    V.tensor_tensor(rel[:, :, :], opq[:, O, :, 0:TN], kv[:, 0, :, :],
                                    ALU.subtract).then_inc(s_rel, 1)
                if wkv:
                    dve.wait_ge(s_rel, s.count(WKV_LAG, 1, 1))
                    for kind, op in ((STATE_W, ALU.min), (TOKEN_W, ALU.max)):
                        for m in range(M):
                            V.tensor_scalar(ex[:, kind, m, :], rel[:, m, :], decay[:, m:m + 1], 0.0, ALU.add,
                                            op).then_inc(s_arg, 1)
                update(s, 0)
                if s.live(0):
                    prev = xt_cols(s, 0, 0)
                    dve.wait_ge(s_diff, s.count(0, 1, 1))
                    dve.wait_ge(s_kvr, s.count(0, 6))
                    for w in range(3):
                        for m in range(M):
                            V.scalar_tensor_tensor(out=mixed[:, w, m, :], in0=diff[:, m, :],
                                                   scalar=vecs[:, MIX + M * w + m:MIX + M * w + m + 1],
                                                   in1=prev[:, m, :], op0=ALU.mult, op1=ALU.add
                                                   ).then_inc(s_mix, 1)
                if o:
                    dve.wait_ge(s_rec, s.count(OUT_LAG, 1, 1))
                    dve.wait_ge(s_numr, s.count(OUT_LAG, 1, 1))
                    dve.wait_ge(s_proj, s.count(OUT_LAG, 2))
                    V.tensor_tensor(y[:, :, :], num[:, :, :], rec[:, :, :], ALU.mult).then_inc(s_y, 1)
                if wkv:
                    dve.wait_ge(s_ex, s.count(WKV_LAG, 3, 2))
                    if s.live(0):
                        dve.wait_ge(s_st[0], s.count(0, M, M))
                    dve.wait_ge(s_kv, s.count(WKV_LAG, 2 * M, 2 * M))
                    V.tensor_tensor(b2v[:, :, :], ex[:, TOKEN_W, :, :], kv[:, 1, :, :], ALU.mult).then_inc(s_b2v, 1)
                    for m in range(M):
                        V.tensor_tensor_scan(opq[:, Q, m, 1:1 + TN], ex[:, STATE_W, m, :], ex[:, TOKEN_W, m, :],
                                             opq[:, Q, m, 0:1], ALU.mult, ALU.add).then_inc(s_q, 1)
                    dve.wait_ge(s_b2v, s.count(WKV_LAG, 1, 1))
                    for m in range(M):
                        V.tensor_tensor_scan(opq[:, PN, m, 1:1 + TN], ex[:, STATE_W, m, :], b2v[:, m, :],
                                             opq[:, PN, m, 0:1], ALU.mult, ALU.add).then_inc(s_p, 1)
                if o:
                    dve.wait_ge(s_add, s.count(OUT_LAG, 1))
                    for h in range(2):
                        dve.wait_ge(s_ot, s.count(OUT_LAG, 2, h + 1))
                        V.scalar_tensor_tensor(out=gate[:, 2 * h:2 * h + 2, :], in0=o_tanh[:, 2 * h:2 * h + 2, :],
                                               scalar=1.0, in1=tok[:, 2 * h:2 * h + 2, :], op0=ALU.add,
                                               op1=ALU.mult).then_inc(s_gate, 1)
                if wkv:
                    dve.wait_ge(s_ex, s.count(WKV_LAG, 3, 3))
                    dve.wait_ge(s_q, s.count(WKV_LAG, M, M))
                    dve.wait_ge(s_ln, s.count(WKV_LAG, 1))
                    V.tensor_tensor(den[:, :, :], ex[:, STATE_Y, :, :], opq[:, Q, :, 0:TN],
                                    ALU.mult).then_inc(s_aq, 1)
                    dve.wait_ge(s_p, s.count(WKV_LAG, M, M))
                    if o:
                        dve.wait_ge(s_y, s.count(OUT_LAG, 1, 1))
                    V.tensor_tensor(num[:, :, :], ex[:, STATE_Y, :, :], opq[:, PN, :, 0:TN],
                                    ALU.mult).then_inc(s_ap, 1)
                    dve.wait_ge(s_aq, s.count(WKV_LAG, 1, 1))
                    V.tensor_tensor(den[:, :, :], ex[:, TOKEN_Y, :, :], den[:, :, :], ALU.add).then_inc(s_den, 1)
                    V.tensor_tensor(b2v[:, :, :], ex[:, TOKEN_Y, :, :], kv[:, 1, :, :], ALU.mult).then_inc(s_bv, 1)
                    dve.wait_ge(s_ap, s.count(WKV_LAG, 1, 1))
                    V.tensor_copy(opq[:, :, :, 0:1], opq[:, :, :, TN:TN + 1]).then_inc(s_carry, 1)
                    dve.wait_ge(s_bv, s.count(WKV_LAG, 1, 1))
                    V.tensor_tensor(num[:, :, :], num[:, :, :], b2v[:, :, :], ALU.add).then_inc(s_num, 1)
                    dve.wait_ge(s_num, s.count(WKV_LAG, 1, 1))
                    dve.wait_ge(s_rt, s.count(WKV_LAG, 1, 1))
                    V.scalar_tensor_tensor(out=num[:, :, :], in0=r_tanh[:, :, :], scalar=1.0, in1=num[:, :, :],
                                           op0=ALU.add, op1=ALU.mult).then_inc(s_numr, 1)
                if o:
                    for h in range(2):
                        dve.wait_ge(s_proj, s.count(OUT_LAG, 2, h + 1))
                        V.tensor_tensor(gate[:, 2 * h:2 * h + 2, :], tok[:, 2 * h:2 * h + 2, :],
                                        gate[:, 2 * h:2 * h + 2, :], ALU.mult).then_inc(s_z, 1)
            run_slots(dve, slot_body)

        @block.tensor
        def _(pe):
            mm = nc.tensor.matmul
            pe.wait_ge(s_ident, 1)

            def layer1(c, round_start, src, ready=None):
                if ready:
                    pe.wait_ge(*ready)
                pe.wait_ge(s_th[c], round_start(c, 1, 0))
                for m in range(M):
                    for k in range(M):
                        last = mm(ps[:, 2 * c + m, :], w_c1[:, k, m * P:(m + 1) * P], src[:, k, :],
                                  start=(k == 0), stop=(k == M - 1))
                    last.then_inc(s_h1[c], 1)

            def layer2(c, round_start):
                pe.wait_ge(s_g1[c], round_start(c, M, M))
                for k in range(M):
                    last = mm(ps[:, 2 * c, :], w_c2[:, k, :], h1[c][:, k, :], start=(k == 0), stop=(k == M - 1))
                last.then_inc(s_h2[c], 1)

            def layer3(c, round_start):
                pe.wait_ge(s_g2[c], round_start(c, 1, 1))
                mm(ps[0:D3, 2 * c + 1, :], w_c3[:, :], h2[c][:, :], start=True, stop=True).then_inc(s_h3[c], 1)

            def logits(c, round_start):
                pe.wait_ge(s_g3[c], round_start(c, 1, 1))
                mm(ps[:, 2 * c, :], w_c4[0:D3, :], h3[c][0:D3, :], start=True, stop=True).then_inc(s_lg[c], 1)

            def prologue_round(c, per_round, k):
                return k

            def prologue_net(step):
                for layer, t in PROLOGUE_NET.get(step, ()):
                    if layer == 0:
                        layer1(t, prologue_round, prologue_cols(t), (s_xe, M * (t + 1)))
                    else:
                        (layer2, layer3)[layer - 1](t, prologue_round)

            for g in range(NT):
                pe.wait_ge(s_xn_v, g + 1)
                pe.wait_ge(s_xn_p, g + 1)
                pe.wait_ge(s_xn_s, 2 * (g + 1))
                for m in range(M):
                    if g >= 1:
                        pe.wait_ge(s_xe, M * (g - 1) + m + 1)
                    for k in range(SUB):
                        last = nc.tensor.transpose(ps[:, KVR_BANK + m, k * P:(k + 1) * P],
                                                   xn_stage[:, g % 2, k, m * P:(m + 1) * P], ident[:, :])
                    last.then_inc(s_xt, 1)
                if g == 0:
                    pe.wait_ge(s_wc, 16 * 4)
                prologue_net(g)
            pe.wait_ge(s_wg, 16 * 3)
            pe.wait_ge(s_mean, 1)
            for m in range(M):
                last = mm(ps[:, KVR_BANK, 0:1], w_g1[:, m, :], ctx_mean[:, m:m + 1], start=(m == 0), stop=(m == 1))
            last.then_inc(s_gp, 1)
            logits(0, prologue_round)
            pe.wait_ge(s_ga, 1)
            mm(ps[0:D3, KVR_BANK, 1:2], w_g2[:, :], g_h1[:, :], start=True, stop=True).then_inc(s_gp, 1)
            logits(1, prologue_round)
            pe.wait_ge(s_ga, 2)
            mm(ps[:, KVR_BANK, 2:3], w_g3[0:D3, :], g_h2[0:D3, :], start=True, stop=True).then_inc(s_gp, 1)
            logits(2, prologue_round)
            pe.wait_ge(s_wt, 16 * 4)
            pe.wait_ge(s_const, 8)

            def project_kvr(s):
                if s.live(WKV_LAG):
                    for w in range(3):
                        pe.wait_ge(s_mix, s.count(WKV_LAG, 3 * M, M * (w + 1)))
                        for m in range(M):
                            if w == 0:
                                pe.wait_ge(s_z, s.count(OUT_LAG, 2))
                            else:
                                pe.wait_ge(s_kv, s.count(WKV_LAG, 2 * M, M * (w - 1) + m + 1))
                            for k in range(M):
                                last = mm(ps[:, KVR_BANK + m, :], w_kvr[:, w, k, m * P:(m + 1) * P],
                                          mixed[:, w, k, :], start=(k == 0), stop=(k == M - 1))
                            last.then_inc(s_kvr, 1)

            def slot_body(s):
                o = s.live(OUT_LAG)
                nets = [c for c in (2, 1, 0) if s.live(NET_LAG[c])]
                project_kvr(s)
                if 2 in nets:
                    layer1(2, s.round, state[1], (s_st[1], s.count(1, M, M)))
                if 0 in nets:
                    layer1(0, s.round, xt_cols(s, NET_LAG[0]))
                if o:
                    pe.wait_ge(s_st[2], s.count(OUT_LAG, M, M))
                    for h in range(2):
                        pe.wait_ge(s_r, s.count(WKV_LAG, M, h + 1))
                        pe.wait_ge(s_z, s.count(OUT_LAG, 2))
                        for k in (2 * h, 2 * h + 1):
                            for m in range(M):
                                last = nc.tensor.transpose(tok[:, k, m * P:(m + 1) * P],
                                                           state[2][:, m, k * P:(k + 1) * P], ident[:, :])
                        last.then_inc(s_tp, 1)
                if 1 in nets:
                    layer1(1, s.round, state[0], (s_st[0], s.count(0, M, M)))
                for c in nets:
                    layer2(c, s.round)
                if o:
                    pe.wait_ge(s_y, s.count(OUT_LAG, 1, 1))
                    for h in range(2):
                        pe.wait_ge(s_gate, s.count(OUT_LAG, 2, h + 1))
                        for k in (2 * h, 2 * h + 1):
                            for m in range(M):
                                last = mm(tok[:, k, :], y[:, m, k * P:(k + 1) * P], w_o[:, m, :],
                                          start=(m == 0), stop=(m == M - 1))
                        last.then_inc(s_proj, 1)
                for layer in (layer3, logits):
                    for c in nets:
                        layer(c, s.round)
            run_slots(pe, slot_body)


def kernel(**inputs):
    import numpy as np
    import concourse.bacc as bacc
    from concourse import mybir as _mybir
    from concourse.bass_utils import run_bass_kernel_spmd as run

    a = {k: np.asarray(v) for k, v in inputs.items()}
    x = a["L0_attn_x"]
    T, C = x.shape[1:]

    def chunks(v):
        return np.ascontiguousarray(v.reshape(-1, P).T)

    vec = np.zeros((P, NVEC), np.float32)
    vec[:, DECAY:DECAY + 2] = chunks(a["L0_attn_time_decay"])
    vec[:, FIRST:FIRST + 2] = chunks(a["L0_attn_time_first"])
    for i, n in enumerate("kvr"):
        vec[:, MIX + 2 * i:MIX + 2 * i + 2] = chunks(a[f"L0_attn_time_mix_{n}"])
    vec[:, CN_B1:CN_B1 + 2] = chunks(a["L0_ffn_cn_b1"])
    vec[:, CN_B2] = a["L0_ffn_cn_b2"]
    vec[0:64, CN_B3] = a["L0_ffn_cn_b3"]
    vec[:, CN_B4] = a["L0_ffn_cn_b4"]
    vec[:, GC_B1] = a["L0_ffn_gc_b1"]
    vec[0:64, GC_B2] = a["L0_ffn_gc_b2"]
    vec[:, GC_B3] = a["L0_ffn_gc_b3"]
    vec[:, RANGE] = a["L0_ffn_adaptive_range"]
    vec[0:64, SIGN] = 1.0
    vec[64:P, SIGN] = -1.0

    arrays = {
        "x": x.reshape(T, C), "vec": vec,
        "wk_t": a["L0_attn_Wk"].T, "wv_t": a["L0_attn_Wv"].T, "wr_t": a["L0_attn_Wr"].T, "wo_t": a["L0_attn_Wo"].T,
        "cn_w1": a["L0_ffn_cn_w1"], "cn_w2": a["L0_ffn_cn_w2"], "cn_w3": a["L0_ffn_cn_w3"],
        "cn_w4": np.repeat(a["L0_ffn_cn_w4"], P, axis=1),
        "gc_w1": a["L0_ffn_gc_w1"], "gc_w2": a["L0_ffn_gc_w2"],
        "gc_w3": np.repeat(a["L0_ffn_gc_w3"], P, axis=1),
    }
    arrays = {k: np.ascontiguousarray(v) for k, v in arrays.items()}
    nc = bacc.Bacc("TRN2", target_bir_lowering=False, num_devices=1)
    args = [nc.dram_tensor(k, v.shape, _mybir.dt.from_np(v.dtype), kind="ExternalInput").ap()
            for k, v in arrays.items()]
    out = nc.dram_tensor("out", (T, C), F32, kind="ExternalOutput").ap()
    rwkv_coupled_ffn(nc, *args, out)
    r = run(nc, [arrays], core_ids=[0])
    return r.results[0]["out"].reshape(1, T, C)
```

```python
from contextlib import ExitStack

import concourse.bass as bass
from concourse import mybir

F32 = mybir.dt.float32
F32R = mybir.dt.float32r
ALU = mybir.AluOpType
ACT = mybir.ActivationFunctionType
AX_X = mybir.AxisListType.X

P = 128
EXP_LN_SET = "natural_log_exp_and_others"
LN_EPS = 1e-5
NEG_INF = -1e38
BASE_COUPLING = 0.1
CYCLES = 3
AHEAD = CYCLES
NET_LAG = (-AHEAD, 0, 1)
MIX_LAG = -1
WKV_LAG = 0
Y_LAG = 1
OUT_LAG = 2
TANH_RING = AHEAD + 1

DECAY, FIRST, MIX, CN_B1, CN_B2, CN_B3, CN_B4, GC_B1, GC_B2, GC_B3, RANGE, SIGN, NVEC = (
    0, 2, 4, 10, 12, 13, 14, 15, 16, 17, 18, 19, 20)


class Slot:

    def __init__(self, tiles, base, reg=None):
        self.tiles, self.base, self.reg = tiles, base, reg

    def live(self, lag):
        return 0 <= self.base - lag < self.tiles

    def count(self, lag, per_tile, k=0):
        const = per_tile * (self.base - lag) + k
        if self.reg is None:
            return max(0, min(const, per_tile * self.tiles))
        assert const > 0
        return self.reg * per_tile + const

    def round(self, chain, per_round, k=0):
        const = per_round * (self.base - max(NET_LAG[chain], 0) + 1) + k
        return const if self.reg is None else self.reg * per_round + const

    def tile(self, lag):
        return self.base - lag if self.reg is None else self.reg + (self.base - lag)


def rwkv_coupled_ffn(nc, x, vec, wk_t, wv_t, wr_t, wo_t, cn_w1, cn_w2, cn_w3, cn_w4, gc_w1, gc_w2, gc_w3, out):
    T, C = x.shape
    M = C // P
    TN = 512
    NT = T // TN
    SUB = TN // P
    D2 = cn_w2.shape[1]
    D3 = cn_w3.shape[1]
    SLOTS = NT + OUT_LAG
    LOOPS = ((OUT_LAG + 1, NT - AHEAD), (NT - AHEAD, NT + MIX_LAG))
    assert M == 2 and D2 == P and D3 == 64 and SUB * C == 2 * TN

    x_tiles = x.rearrange("(g s p) c -> g p s c", s=SUB, p=P)
    out_tiles = out.rearrange("(g s p) c -> g p s c", s=SUB, p=P)

    with ExitStack() as ctx:
        def sb(name, *shape):
            return ctx.enter_context(nc.sbuf_tensor(name, [P, *shape], F32))

        def sb_split(name, *shape):
            return [ctx.enter_context(nc.sbuf_tensor(f"{name}_{part}", [P, *shape], F32R))
                    for part in ("high", "low")]

        def sem(name):
            return ctx.enter_context(nc.semaphore(name))

        vecs = sb("vecs", NVEC)
        w_kvr = sb("w_kvr", 3, M, C)
        w_r_split = sb_split("w_r", M, C)
        w_o = sb("w_o", M, C)
        w_c1 = sb("w_c1", M, C)
        w_c1_split = sb_split("w_c1", M, C)
        w_c2 = sb("w_c2", M, D2)
        w_c3 = sb("w_c3", D3)
        w_c4 = sb("w_c4", P)
        w_g2 = sb("w_g2", D3)
        w_g3 = sb("w_g3", P)
        ident = sb("ident", P)
        decay_pos = sb("decay_pos", M)
        decay = sb("decay", M)
        neg_first = sb("neg_first", M)
        half_b4 = sb("half_b4", 1)
        half_g3 = sb("half_g3", 1)
        beta = sb("beta", 1)
        alpha = sb("alpha", 1)
        range_sign = sb("range_sign", 1)
        base_sign = sb("base_sign", 1)
        stats = sb("stats", NT, SUB, 6)
        meanvar = sb("meanvar", NT, SUB, 2)
        var_eps = sb("var_eps", NT, SUB)
        power = sb("power", SUB)
        rstd = sb("rstd", NT, SUB)
        shift = sb("shift", NT, SUB)
        tile_sums = sb("tile_sums", M, NT)
        ctx_sum = sb("ctx_sum", M)
        ctx_mean = sb("ctx_mean", M)
        g_h1 = sb("g_h1", 1)
        g_h2 = sb("g_h2", 1)
        g_tanh = sb("g_tanh", 1)
        xt = sb("xt", M, 1 + T)
        diff = sb("diff", M, TN)
        mixed = sb("mixed", 3, M, TN)
        mixed_r_split = sb_split("mixed_r", M, TN)
        kv = sb("kv", 2, M, TN)
        r_tanh = sb("r_tanh", M, TN)
        rel = sb("rel", M, TN)
        ex = sb("ex", 4, M, TN)
        STATE_Y, TOKEN_Y, STATE_W, TOKEN_W = range(4)
        opq = sb("opq", 3, M, 1 + TN)
        b2v = sb("b2v", M, TN)
        den = sb("den", M, TN)
        num = sb("num", M, TN)
        rec = sb("rec", M, TN)
        y = sb("y", M, TN)
        num_r = sb("num_r", M, TN)
        h1 = [sb(f"h1_{c}", M, TN) for c in range(CYCLES)]
        h2 = [h1[c][:, 1, :] for c in range(CYCLES)]
        h3 = [h1[c][:, 0, :] for c in range(CYCLES)]
        tanh_0 = sb("tanh_0", TANH_RING, TN)
        coup = [None] + [sb(f"coup_{c}", TN) for c in range(1, CYCLES)]
        xt_split = sb_split("xt", M, TN)
        turned = [b2v, sb("turned", M, TN)]
        state = [sb(f"state_{c}", M, TN) for c in range(CYCLES)]
        o_tanh = sb("o_tanh", SUB, C)
        gate = sb("gate", SUB, C)
        resid = sb("resid", SUB, C)
        w_g1 = y[:, :, 0:D2]
        last_resid = mixed[:, 0, :, :].rearrange("p m t -> p (m t)").rearrange("p (s c) -> p s c", c=C)
        XS = 4
        x_stage = ex[:, :, :, :].rearrange("p a m t -> p a (m t)").rearrange("p a (s c) -> p a s c", c=C)
        xn_stage = kv[:, :, :, :].rearrange("p a m t -> p a (m t)").rearrange("p a (s c) -> p a s c", c=C)

        ps = ctx.enter_context(nc.psum_tensor("ps", [P, 8, TN], F32))
        KVR_BANK = 2 * CYCLES
        GLOBAL_BANK = 2
        WARM_UP = 5

        def banks_by_token(first):
            return ps[:, first:first + 2, :].rearrange("p b t -> p (b t)").rearrange("p (s c) -> p s c", c=C)

        tok = banks_by_token(KVR_BANK)

        s_vec = sem("vec_loaded")
        s_wc = sem("coupling_weights_loaded")
        s_wg = sem("global_weights_loaded")
        s_wt = sem("rwkv_weights_loaded")
        s_x = [sem(f"x_loaded_{i}") for i in range(XS)]
        s_x0 = [sem(f"x_tile_0_half_{h}_loaded") for h in range(2)]
        s_zero = sem("ident_zeroed")
        s_ident = sem("ident_ready")
        s_init = sem("carries_ready")
        s_decay = sem("decay_ready")
        s_const = sem("constants_ready")
        s_power = sem("power_ready")
        s_stat = sem("stats_done")
        s_mv = sem("meanvar_done")
        s_ve = sem("variance_plus_eps_done")
        s_rstd = sem("rstd_done")
        s_shift = sem("shift_done")
        s_xn_v = sem("xn_vector_done")
        s_xn_s = sem("xn_scalar_done")
        s_xn_p = sem("xn_pool_done")
        s_xt = sem("xt_transposed")
        s_xe = sem("xt_stored")
        s_split = sem("split_done")
        s_sum = sem("context_summed")
        s_mean = sem("context_mean_done")
        s_gp = sem("global_layer_done")
        s_ga = sem("global_act_done")
        s_alpha = sem("alpha_ready")
        s_diff = sem("diff_done")
        s_mix = sem("mix_done")
        s_rsplit = sem("r_split_done")
        s_kvr = sem("kvr_done")
        s_kv = sem("kv_stored")
        s_r = sem("r_stored")
        s_rt = sem("r_tanh_done")
        s_o = sem("o_scanned")
        s_rel = sem("rel_done")
        s_relu = sem("output_exponents_done")
        s_arg = sem("state_exponents_done")
        s_ex = sem("exps_done")
        s_b2v = sem("b2v_done")
        s_q = sem("q_scanned")
        s_p = sem("p_scanned")
        s_aq = sem("aq_done")
        s_ap = sem("ap_done")
        s_den = sem("den_done")
        s_bv = sem("bv_done")
        s_num = sem("num_done")
        s_numr = sem("num_times_r_done")
        s_carry = sem("carry_done")
        s_ln = sem("ln_done")
        s_rec = sem("rec_done")
        s_y = sem("y_done")
        s_h1 = [sem(f"h1_pre_{c}") for c in range(CYCLES)]
        s_h2 = [sem(f"h2_pre_{c}") for c in range(CYCLES)]
        s_h3 = [sem(f"h3_pre_{c}") for c in range(CYCLES)]
        s_lg = [sem(f"logit_{c}") for c in range(CYCLES)]
        s_g1 = [sem(f"h1_done_{c}") for c in range(CYCLES)]
        s_g2 = [sem(f"h2_done_{c}") for c in range(CYCLES)]
        s_g3 = [sem(f"h3_done_{c}") for c in range(CYCLES)]
        s_th = [sem(f"tanh_done_{c}") for c in range(CYCLES)]
        s_cs = [sem(f"coupling_done_{c}") for c in range(CYCLES)]
        s_mul = [sem(f"turn_done_{c}") for c in range(CYCLES)]
        s_st = [sem(f"state_done_{c}") for c in range(CYCLES)]
        s_tp = sem("out_transposed")
        s_ot = sem("o_tanh_done")
        s_gate = sem("gate_done")
        s_proj = sem("out_projected")
        s_z = sem("gated_done")
        s_xr = sem("residual_loaded")
        s_xl = sem("last_residual_loaded")
        s_add = sem("sum_done")
        s_last = sem("last_sum_done")
        s_out = sem("out_stored")

        def last_round(chain, per_round, k):
            assert chain == 1
            return per_round * (NT + 1) + k

        def half_tile(h):
            return slice(h * TN // 2, (h + 1) * TN // 2)

        def splits_r(s, lag):
            return s.live(lag) and (s.base < 0 or s.live(NET_LAG[0]))

        NET_ORDER = (2, 0, 1)

        def run_slots(eng, slot_body, drain=None):
            for j in range(LOOPS[0][0]):
                slot_body(Slot(NT, j))
            for first, end in LOOPS:
                with eng.Fori(0, end - first) as i:
                    slot_body(Slot(NT, first, i))
            if drain:
                drain(*(Slot(NT, j) for j in range(LOOPS[-1][1], SLOTS)))
            else:
                for j in range(LOOPS[-1][1], SLOTS):
                    slot_body(Slot(NT, j))

        def xt_cols(slot, lag, first=1):
            if slot.reg is None:
                at = (slot.base - lag) * TN + first
                return xt[:, :, at:at + TN]
            return xt[:, :, bass.ds(slot.reg * TN + ((slot.base - lag) * TN + first), TN)]

        def coupling_of(s, lag):
            if s.reg is None:
                return tanh_0[:, s.tile(lag) % TANH_RING, :]
            return tanh_0[:, :, :].rearrange("p r t -> p (r t)")[
                :, bass.ds((s.tile(lag) % TANH_RING) * TN, TN)]

        def is_last(s, lag):
            return s.reg is None and s.tile(lag) == NT - 1

        def wkv_of(s, lag):
            return num if is_last(s, lag) else y

        def reciprocal_of(s):
            return den if is_last(s, Y_LAG) else rec

        def tokens_of(buffer, last_buffer, s):
            if is_last(s, OUT_LAG):
                return last_buffer.rearrange("p m t -> p (m t)").rearrange("p (s c) -> p s c", c=C)
            return buffer

        def o_tanh_of(s):
            return tokens_of(o_tanh, kv[:, 0, :, :], s)

        def gate_of(s):
            return tokens_of(gate, rel[:, :, :], s)

        def projected_tile(s):
            return banks_by_token(4) if is_last(s, OUT_LAG) else tok

        def turned_tile(s):
            if is_last(s, OUT_LAG):
                return banks_by_token(2)
            if s.live(NET_LAG[0]):
                return tok
            return banks_by_token(0)

        def prologue_cols(t):
            return xt[:, :, 1 + t * TN:1 + (t + 1) * TN]

        def source(slot, cycle, lag):
            return xt_cols(slot, lag) if cycle == 0 else state[cycle - 1][:, :, :]

        MIX_AFTER = 2
        PROLOGUE_NET = {1: [(0, 0)], 2: [(0, 1)], 3: [(0, 2)], 4: [(1, 0)], 5: [(1, 1)], 6: [(1, 2)],
                        7: [(2, 0), (2, 1), (2, 2)]}

        block = ctx.enter_context(nc.Block())

        @block.sync
        def _(sp):
            def rows(w):
                return w.rearrange("(k p) n -> p k n", p=P)

            def load_x(g):
                if g >= XS:
                    sp.wait_ge(s_xn_v, g - XS + 1)
                    sp.wait_ge(s_xn_s, 2 * (g - XS + 1))
                    sp.wait_ge(s_xn_p, g - XS + 1)
                sp.dma_start(x_stage[:, g % XS, :, :], x_tiles[g]).then_inc(s_x[g % XS], 16)

            def load_w(dst, src, loaded):
                sp.dma_start(dst, src).then_inc(loaded, 16)

            for h in range(2):
                sp.dma_start(x_stage[:, 0, 2 * h:2 * h + 2, :], x_tiles[0, :, 2 * h:2 * h + 2, :]
                             ).then_inc(s_x0[h], 16)
            sp.dma_start(vecs[:, :], vec).then_inc(s_vec, 16)
            load_x(1)
            load_w(w_c1[:, :, :], rows(cn_w1), s_wc)
            load_x(2)
            load_w(w_c2[:, :, :], rows(cn_w2), s_wc)
            load_x(3)
            load_w(w_c3[:, :], cn_w3, s_wc)
            load_w(w_c4[0:D3, :], cn_w4, s_wc)
            load_x(4)
            load_w(w_g1[:, :, :], rows(gc_w1), s_wg)
            load_w(w_g2[:, :], gc_w2, s_wg)
            load_w(w_g3[0:D3, :], gc_w3, s_wg)
            load_x(5)
            for i, w in enumerate((wk_t, wv_t, wr_t)):
                load_w(w_kvr[:, i, :, :], rows(w), s_wt)
            load_x(6)
            load_w(w_o[:, :, :], rows(wo_t), s_wt)
            load_x(7)

            def slot_body(s):
                if s.live(OUT_LAG):
                    sp.wait_ge(s_out, s.count(OUT_LAG, 16))
                    sp.dma_start(resid[:, :, :], x_tiles[s.tile(OUT_LAG)]).then_inc(s_xr, 16)
                    sp.wait_ge(s_add, s.count(OUT_LAG, 1, 1))
                    sp.dma_start(out_tiles[s.tile(OUT_LAG)], resid[:, :, :]).then_inc(s_out, 16)

            def drain(a, b, c):
                slot_body(a)
                sp.wait_ge(s_kvr, 6 * NT)
                sp.dma_start(last_resid, x_tiles[NT - 1]).then_inc(s_xl, 16)
                slot_body(b)
                for h in range(2):
                    sp.wait_ge(s_last, h + 1)
                    sp.dma_start(out_tiles[NT - 1, :, 2 * h:2 * h + 2, :],
                                 last_resid[:, 2 * h:2 * h + 2, :]).then_inc(s_out, 16)
            run_slots(sp, slot_body, drain)
            sp.wait_ge(s_out, 16 * (NT + 1))

        @block.gpsimd
        def _(pool):
            nc.gpsimd.memset(ident[:, :], 0.0).then_inc(s_zero, 1)
            pool.wait_ge(s_zero, 1)
            nc.gpsimd.affine_select(out=ident[:, :], in_=ident[:, :], compare_op=ALU.not_equal, fill=1.0,
                                    base=0, pattern=[[-1, P]], channel_multiplier=1).then_inc(s_ident, 1)
            nc.gpsimd.memset(xt[:, :, 0:1], 0.0).then_inc(s_init, 1)
            nc.gpsimd.memset(opq[:, 0, :, 0:1], NEG_INF).then_inc(s_init, 1)
            nc.gpsimd.memset(opq[:, 1:3, :, 0:1], 0.0).then_inc(s_init, 1)
            pool.wait_ge(s_init, 3)
            nc.gpsimd.memset(power[:, :], -0.5).then_inc(s_power, 1)
            pool.wait_ge(s_power, 1)

            def inverse_std(g):
                pool.wait_ge(s_mv, SUB * (g + 1))
                nc.gpsimd.tensor_scalar(var_eps[:, g, :], meanvar[:, g, :, 1], 1.0, LN_EPS, ALU.mult,
                                        ALU.add).then_inc(s_ve, 1)
                pool.wait_ge(s_ve, g + 1)
                nc.gpsimd.tensor_tensor(rstd[:, g, :], var_eps[:, g, :], power[:, :], ALU.pow).then_inc(s_rstd, 1)

            def difference(s):
                if s.live(MIX_LAG):
                    pool.wait_ge(s_mix, s.count(MIX_LAG, 3 * M))
                    nc.gpsimd.tensor_tensor(diff[:, :, :], xt_cols(s, MIX_LAG), xt_cols(s, MIX_LAG, 0),
                                            ALU.subtract).then_inc(s_diff, 1)

            inverse_std(0)
            for g in range(NT):
                if 1 <= g < NT - 1:
                    inverse_std(g + 1)
                pool.wait_ge(s_shift, g + 1)
                if g >= 2:
                    pool.wait_ge(s_xt, M * (g - 1))
                nc.gpsimd.tensor_scalar(xn_stage[:, g % 2, 1, :], x_stage[:, g % XS, 1, :], rstd[:, g, 1:2],
                                        shift[:, g, 1:2], ALU.mult, ALU.add).then_inc(s_xn_p, 1)
                if g == 0:
                    inverse_std(1)
                if g == MIX_AFTER:
                    pool.wait_ge(s_xe, M)
                    difference(Slot(NT, MIX_LAG))
            pool.wait_ge(s_xe, M * NT)

            def slot_body(s):
                difference(s)
                if s.live(OUT_LAG) and s.live(OUT_LAG - 1):
                    pool.wait_ge(s_xr, s.count(OUT_LAG, 16, 16))
                    pool.wait_ge(s_z, s.count(OUT_LAG, 2, 2))
                    nc.gpsimd.tensor_tensor(resid[:, :, :], gate[:, :, :], resid[:, :, :],
                                            ALU.add).then_inc(s_add, 1)
            run_slots(pool, slot_body)

        @block.scalar
        def _(act):
            act.wait_ge(s_vec, 16)
            nc.scalar.activation(decay_pos[:, :], vecs[:, DECAY:DECAY + M], ACT.Exp).then_inc(s_decay, 1)

            def gelu1(c, round_start, chunks=range(M)):
                for m in chunks:
                    act.wait_ge(s_h1[c], round_start(c, M, m + 1))
                    nc.scalar.activation(h1[c][:, m, :], ps[:, 2 * c + m, :], ACT.Gelu,
                                         bias=vecs[:, CN_B1 + m:CN_B1 + m + 1]).then_inc(s_g1[c], 1)

            def gelu2(c, round_start):
                act.wait_ge(s_h2[c], round_start(c, 1, 1))
                nc.scalar.activation(h2[c], ps[:, 2 * c, :], ACT.Gelu,
                                     bias=vecs[:, CN_B2:CN_B2 + 1]).then_inc(s_g2[c], 1)

            def gelu3(c, round_start):
                act.wait_ge(s_h3[c], round_start(c, 1, 1))
                nc.scalar.activation(h3[c][0:D3, :], ps[0:D3, 2 * c + 1, :], ACT.Gelu,
                                     bias=vecs[0:D3, CN_B3:CN_B3 + 1]).then_inc(s_g3[c], 1)

            def tanh_logit(c, round_start, dst):
                act.wait_ge(s_lg[c], round_start(c, 1, 1))
                nc.scalar.activation(dst, ps[:, 2 * c, :], ACT.Tanh, scale=0.5,
                                     bias=half_b4[:, :]).then_inc(s_th[c], 1)

            def prologue_round(c, per_round, k):
                return k

            def normalise(g):
                act.wait_ge(s_shift, g + 1)
                if g >= 2:
                    act.wait_ge(s_xt, M * (g - 1))
                for k in range(SUB // 2, SUB):
                    nc.scalar.activation(xn_stage[:, g % 2, k, :], x_stage[:, g % XS, k, :], ACT.Identity,
                                         bias=shift[:, g, k:k + 1], scale=rstd[:, g, k:k + 1]
                                         ).then_inc(s_xn_s, 1)

            def store_xt(g):
                for m in range(M):
                    act.wait_ge(s_xt, M * g + m + 1)
                    nc.scalar.activation(xt[:, m, 1 + g * TN:1 + (g + 1) * TN], ps[:, KVR_BANK + m, :],
                                         ACT.Identity, accum_out=tile_sums[:, m, g:g + 1]).then_inc(s_xe, 1)

            nc.scalar.preload_act_table(ACT.Gelu)
            normalise(0)
            for g in range(NT):
                if g + 1 < NT:
                    normalise(g + 1)
                store_xt(g)
                for layer, t in PROLOGUE_NET.get(g, ()):
                    (gelu1, gelu2, gelu3)[layer](t, prologue_round)
            def store_k(s, m):
                act.wait_ge(s_kvr, s.count(WKV_LAG, 6, m + 1))
                act.wait_ge(s_rel, s.count(WKV_LAG, 1))
                nc.scalar.copy(kv[:, 0, m, :], ps[:, KVR_BANK + m, :]).then_inc(s_kv, 1)

            act.wait_ge(s_const, 7)
            act.wait_ge(s_gp, 1)
            nc.scalar.activation(g_h1[:, :], ps[:, GLOBAL_BANK, 0:1], ACT.Gelu,
                                 bias=vecs[:, GC_B1:GC_B1 + 1]).then_inc(s_ga, 1)
            tanh_logit(0, prologue_round, tanh_0[:, 0, :])
            act.wait_ge(s_gp, 2)
            nc.scalar.activation(g_h2[0:D3, :], ps[0:D3, GLOBAL_BANK, 1:2], ACT.Gelu,
                                 bias=vecs[0:D3, GC_B2:GC_B2 + 1]).then_inc(s_ga, 1)
            tanh_logit(2, prologue_round, tanh_0[:, 2, :])
            act.wait_ge(s_gp, 3)
            nc.scalar.activation(g_tanh[:, :], ps[:, GLOBAL_BANK, 2:3], ACT.Tanh, scale=0.5,
                                 bias=half_g3[:, :]).then_inc(s_ga, 1)
            store_k(Slot(NT, 0), 0)
            store_k(Slot(NT, 0), 1)
            tanh_logit(1, prologue_round, tanh_0[:, 1, :])
            act.wait_ge(s_alpha, 2)
            for c in range(1, CYCLES):
                act.wait_ge(s_th[c], 1)

            def coupling(s, c):
                lag = max(NET_LAG[c], 0)
                if s.live(lag):
                    if c == 0:
                        act.wait_ge(s_th[0], max(1, s.base - AHEAD + 2) + (0 if s.reg is None else s.reg))
                        factor = coupling_of(s, 0)
                    else:
                        act.wait_ge(s_th[c], s.round(c, 1, 1))
                        factor = coup[c][:, :]
                    nc.scalar.activation(factor, factor, ACT.Identity, scale=beta[:, :],
                                         bias=alpha[:, :]).then_inc(s_cs[c], 1)

            def store_v(s, m):
                if s.live(WKV_LAG):
                    act.wait_ge(s_kvr, s.count(WKV_LAG, 6, M + m + 1))
                    act.wait_ge(s_bv, s.count(WKV_LAG, 1))
                    nc.scalar.copy(kv[:, 1, m, :], ps[:, KVR_BANK + m, :]).then_inc(s_kv, 1)

            def log_den(s):
                if s.live(Y_LAG):
                    act.wait_ge(s_den, s.count(Y_LAG, 1, 1))
                    if not is_last(s, Y_LAG):
                        act.wait_ge(s_y, s.count(Y_LAG, 1))
                    nc.scalar.activation(reciprocal_of(s)[:, :, :], den[:, :, :], ACT.Ln).then_inc(s_ln, 1)

            def reciprocal(s):
                if s.live(Y_LAG):
                    act.wait_ge(s_ln, s.count(Y_LAG, 1, 1))
                    nc.scalar.activation(reciprocal_of(s)[:, :, :], reciprocal_of(s)[:, :, :], ACT.Exp,
                                         scale=-1.0).then_inc(s_rec, 1)

            def output_exponents(s):
                if s.live(WKV_LAG):
                    act.wait_ge(s_rel, s.count(WKV_LAG, 1, 1))
                    for m in range(M):
                        nc.scalar.activation(ex[:, STATE_Y, m, :], rel[:, m, :], ACT.Relu, scale=-1.0,
                                             bias=vecs[:, FIRST + m:FIRST + m + 1]).then_inc(s_relu, 1)
                        nc.scalar.activation(ex[:, TOKEN_Y, m, :], rel[:, m, :], ACT.Relu,
                                             bias=neg_first[:, m:m + 1]).then_inc(s_relu, 1)

            def store_r(s):
                if s.live(WKV_LAG):
                    for m in range(M):
                        act.wait_ge(s_kvr, s.count(WKV_LAG, 6, 2 * M + m + 1))
                        act.wait_ge(s_numr, s.count(WKV_LAG, 1))
                        nc.scalar.copy(r_tanh[:, m, :], ps[:, KVR_BANK + m, :]).then_inc(s_r, 1)

            def exponentials(s):
                if s.live(WKV_LAG):
                    for i, (kind, scale) in enumerate(((STATE_W, 1.0), (TOKEN_W, -1.0))):
                        act.wait_ge(s_arg, s.count(WKV_LAG, 2 * M, M * (i + 1)))
                        nc.scalar.activation(ex[:, kind, :, :], ex[:, kind, :, :], ACT.Exp,
                                             scale=scale).then_inc(s_ex, 1)
                    act.wait_ge(s_relu, s.count(WKV_LAG, 2 * M, 2 * M))
                    nc.scalar.activation(ex[:, 0:2, :, :], ex[:, 0:2, :, :], ACT.Exp, scale=-1.0).then_inc(s_ex, 1)

            def tanh_r(s):
                if s.live(WKV_LAG):
                    act.wait_ge(s_r, s.count(WKV_LAG, M, M))
                    nc.scalar.activation(r_tanh[:, :, :], r_tanh[:, :, :], ACT.Tanh, scale=0.5).then_inc(s_rt, 1)

            def tanh_out(s):
                if s.live(OUT_LAG):
                    for h in range(2):
                        act.wait_ge(s_tp, s.count(OUT_LAG, 2, h + 1))
                        if not is_last(s, OUT_LAG):
                            act.wait_ge(s_gate, s.count(OUT_LAG, 2))
                        nc.scalar.activation(o_tanh_of(s)[:, 2 * h:2 * h + 2, :], turned_tile(s)[:, 2 * h:2 * h + 2, :],
                                             ACT.Tanh, scale=0.5).then_inc(s_ot, 1)

            def exp_session(s):
                if s.live(WKV_LAG) or s.live(Y_LAG):
                    nc.scalar.preload_act_table_set(EXP_LN_SET)
                    store_v(s, 0)
                    log_den(s)
                    store_v(s, 1)
                    reciprocal(s)
                    output_exponents(s)
                    store_r(s)
                    exponentials(s)
                    nc.scalar.preload_act_table(ACT.Gelu)

            def slot_body(s):
                nets = [c for c in NET_ORDER if s.live(NET_LAG[c])]
                if s.base > 0:
                    for m in range(M):
                        store_k(s, m)
                coupling(s, 0)
                exp_session(s)
                for c in (2, 0):
                    if c in nets:
                        gelu1(c, s.round)
                tanh_out(s)
                if 1 in nets:
                    gelu1(1, s.round)
                tanh_r(s)
                if splits_r(s, MIX_LAG):
                    act.wait_ge(s_mix, s.count(MIX_LAG, 3 * M, 3 * M))
                    act.wait_ge(s_kvr, s.count(MIX_LAG, 6))
                    act.wait_ge(s_rsplit, s.count(MIX_LAG, 2, 2))
                    nc.scalar.copy(mixed_r_split[0][:, :, :], mixed[:, 2, :, :]).then_inc(s_rsplit, 1)
                for layer in (gelu2, gelu3):
                    for c in nets:
                        layer(c, s.round)
                for c in nets:
                    if c == 0:
                        act.wait_ge(s_mul[0], s.count(0, 1))
                    elif s.live(c):
                        act.wait_ge(s_mul[c], s.count(c, 1, 1))
                    tanh_logit(c, s.round, coup[c][:, :] if c else coupling_of(s, NET_LAG[0]))
                for c in (2, 1):
                    coupling(s, c)

            def drain(a, b, c):
                for m in range(M):
                    store_k(a, m)
                coupling(a, 0)
                exp_session(a)
                gelu1(1, a.round)
                gelu1(2, a.round)
                gelu2(1, a.round)
                tanh_out(a)
                gelu3(1, a.round)
                gelu2(2, a.round)
                act.wait_ge(s_mul[1], NT - 1)
                tanh_logit(1, a.round, coup[1][:, :])
                coupling(a, 1)
                gelu3(2, a.round)
                exp_session(b)
                gelu1(1, last_round, (0,))
                tanh_r(a)
                act.wait_ge(s_mul[2], NT - 2)
                tanh_logit(2, a.round, coup[2][:, :])
                gelu1(1, last_round, (1,))
                coupling(a, 2)
                gelu2(1, last_round)
                gelu3(1, last_round)
                tanh_out(b)
                act.wait_ge(s_mul[1], NT)
                tanh_logit(1, last_round, coup[1][:, :])
                for h in range(2):
                    act.wait_ge(s_th[1], last_round(1, 1, 1))
                    act.wait_ge(s_mul[2], NT - 1)
                    nc.scalar.activation(coup[2][:, half_tile(h)], coup[1][:, half_tile(h)], ACT.Identity,
                                         scale=beta[:, :], bias=alpha[:, :]).then_inc(s_cs[2], 1)
                tanh_out(c)
            run_slots(act, slot_body, drain)

        @block.vector
        def _(dve):
            V = nc.vector
            def derived_vectors():
                dve.wait_ge(s_vec, 16)
                V.tensor_scalar(neg_first[:, :], vecs[:, FIRST:FIRST + M], -1.0, None, ALU.mult).then_inc(s_const, 1)
                V.tensor_scalar(half_b4[:, :], vecs[:, CN_B4:CN_B4 + 1], 0.5, None, ALU.mult).then_inc(s_const, 1)
                V.tensor_scalar(half_g3[:, :], vecs[:, GC_B3:GC_B3 + 1], 0.5, None, ALU.mult).then_inc(s_const, 1)
                V.tensor_tensor(range_sign[:, :], vecs[:, RANGE:RANGE + 1], vecs[:, SIGN:SIGN + 1],
                                ALU.mult).then_inc(s_const, 1)
                V.tensor_scalar(base_sign[:, :], vecs[:, SIGN:SIGN + 1], BASE_COUPLING, None,
                                ALU.mult).then_inc(s_const, 1)
                dve.wait_ge(s_const, 4)
                V.tensor_scalar(beta[:, :], range_sign[:, :], 0.3, None, ALU.mult).then_inc(s_const, 1)
                dve.wait_ge(s_decay, 1)
                V.tensor_scalar(decay[:, :], decay_pos[:, :], -1.0, None, ALU.mult).then_inc(s_const, 1)

            def tile_stats(g):
                if g:
                    dve.wait_ge(s_x[g % XS], 16 * (g // XS + (g % XS > 0)))
                for k in range(SUB):
                    if g == 0 and k % 2 == 0:
                        dve.wait_ge(s_x0[k // 2], 16)
                    V.bn_stats(stats[:, g, k, :], x_stage[:, g % XS, k, :]).then_inc(s_stat, 1)
                for k in range(SUB):
                    dve.wait_ge(s_stat, SUB * g + k + 1)
                    V.bn_aggr(meanvar[:, g, k, :], stats[:, g, k, :]).then_inc(s_mv, 1)

            def tile_shift(g):
                dve.wait_ge(s_rstd, g + 1)
                V.scalar_tensor_tensor(out=shift[:, g, :], in0=meanvar[:, g, :, 0], scalar=-1.0,
                                       in1=rstd[:, g, :], op0=ALU.mult, op1=ALU.mult).then_inc(s_shift, 1)

            def split(parts, whole, done, high_done):
                high, low = [part[:, :, :] for part in parts]
                V.tensor_copy(high, whole).then_inc(done, 1)
                dve.wait_ge(done, high_done)
                V.tensor_tensor(low, whole, high.bitcast(F32), ALU.subtract).then_inc(done, 1)

            def split_r(s):
                if splits_r(s, MIX_LAG):
                    if s.base < 0:
                        dve.wait_ge(s_mix, 3 * M)
                        split(mixed_r_split, mixed[:, 2, :, :], s_rsplit, 3)
                    else:
                        dve.wait_ge(s_rsplit, s.count(MIX_LAG, 2, 3))
                        V.tensor_tensor(mixed_r_split[1][:, :, :], mixed[:, 2, :, :],
                                        mixed_r_split[0][:, :, :].bitcast(F32), ALU.subtract
                                        ).then_inc(s_rsplit, 1)

            def mix(s, projections=range(3)):
                if s.live(MIX_LAG):
                    prev = xt_cols(s, MIX_LAG, 0)
                    dve.wait_ge(s_diff, s.count(MIX_LAG, 1, 1))
                    for w in projections:
                        dve.wait_ge(s_kvr, max(0, s.count(MIX_LAG, 6, 2 * w - 4)) if s.reg is None else
                                    s.count(MIX_LAG, 6, 2 * w - 4))
                        for m in range(M):
                            V.scalar_tensor_tensor(out=mixed[:, w, m, :], in0=diff[:, m, :],
                                                   scalar=vecs[:, MIX + M * w + m:MIX + M * w + m + 1],
                                                   in1=prev[:, m, :], op0=ALU.mult, op1=ALU.add
                                                   ).then_inc(s_mix, 1)

            def split_xt(s):
                if s.live(NET_LAG[0]):
                    dve.wait_ge(s_h1[0], s.round(0, M))
                    split(xt_split, xt_cols(s, NET_LAG[0]), s_split, s.round(0, 2, 1))

            tile_stats(0)
            tile_stats(1)
            tile_shift(0)
            for g in range(NT):
                if g == 1:
                    derived_vectors()
                if 1 <= g < NT - 1:
                    tile_stats(g + 1)
                if g:
                    tile_shift(g)
                if g >= 2:
                    dve.wait_ge(s_xt, M * (g - 1))
                V.tensor_scalar(xn_stage[:, g % 2, 0, :], x_stage[:, g % XS, 0, :], meanvar[:, g, 0, 0:1],
                                rstd[:, g, 0:1], ALU.subtract, ALU.mult).then_inc(s_xn_v, 1)
                if g == MIX_AFTER + 4:
                    dve.wait_ge(s_wc, 16 * 4)
                    split(w_c1_split, w_c1[:, :, :], s_split, 1)
                    dve.wait_ge(s_wt, 16 * 4)
                    split(w_r_split, w_kvr[:, 2, :, :], s_rsplit, 1)
                    split_r(Slot(NT, MIX_LAG))
                if MIX_AFTER < g <= MIX_AFTER + 3:
                    mix(Slot(NT, MIX_LAG), (g - MIX_AFTER - 1,))

            dve.wait_ge(s_wt, 16 * 4)
            V.tensor_scalar(w_o[:, :, :], w_o[:, :, :], 0.25, None, ALU.mult).then_inc(s_const, 1)
            dve.wait_ge(s_xe, M * NT)
            V.tensor_reduce(ctx_sum[:, :], tile_sums[:, :, :], AX_X, ALU.add).then_inc(s_sum, 1)
            dve.wait_ge(s_sum, 1)
            V.tensor_scalar(ctx_mean[:, :], ctx_sum[:, :], 1.0 / T, None, ALU.mult).then_inc(s_mean, 1)
            dve.wait_ge(s_ga, 3)
            V.tensor_tensor(alpha[:, :], range_sign[:, :], g_tanh[:, :], ALU.mult).then_inc(s_alpha, 1)
            dve.wait_ge(s_alpha, 1)
            V.scalar_tensor_tensor(out=alpha[:, :], in0=alpha[:, :], scalar=0.7, in1=base_sign[:, :],
                                   op0=ALU.mult, op1=ALU.add).then_inc(s_alpha, 1)

            def update(s, c):
                lag = c
                if s.live(lag):
                    src = source(s, c, lag)
                    dst = h1[0] if c == 1 and s.reg is None and s.tile(lag) == NT - 1 else state[c]
                    dve.wait_ge(s_cs[c], s.count(lag, 1, 1))
                    if c:
                        dve.wait_ge(s_st[c - 1], s.count(lag, M, M))
                    if c == 0 and s.live(OUT_LAG):
                        dve.wait_ge(s_st[2], s.count(OUT_LAG, M, M))
                    tu = turned[c % 2]
                    factor = coup[c][:, :] if c else coupling_of(s, 0)
                    V.tensor_tensor(tu[:, :, :], factor.unsqueeze(1).to_broadcast([P, M, TN]), src,
                                    ALU.mult).then_inc(s_mul[c], 1)
                    dve.wait_ge(s_mul[c], s.count(lag, 1, 1))
                    if dst is h1[0]:
                        dve.wait_ge(s_h2[0], NT - AHEAD + 1)
                    elif c + 1 < CYCLES:
                        dve.wait_ge(s_h1[c + 1], s.count(lag, M, M))
                        if s.live(lag + 1):
                            dve.wait_ge(s_st[c + 1], s.count(lag + 1, M, M))
                    else:
                        dve.wait_ge(s_tp, s.count(lag, 2))
                    V.tensor_tensor(dst[:, 0, :], src[:, 0, :], tu[:, 1, :], ALU.add).then_inc(s_st[c], 1)
                    V.tensor_tensor(dst[:, 1, :], src[:, 1, :], tu[:, 0, :], ALU.subtract).then_inc(s_st[c], 1)

            O, PN, Q = 0, 1, 2

            def maxima(s):
                if s.live(WKV_LAG):
                    for m in range(M):
                        dve.wait_ge(s_kv, s.count(WKV_LAG, 2 * M, m + 1))
                        dve.wait_ge(s_carry, s.count(WKV_LAG, 1))
                        V.tensor_tensor_scan(opq[:, O, m, 1:1 + TN], decay[:, m:m + 1].to_broadcast([P, TN]),
                                             kv[:, 0, m, :], opq[:, O, m, 0:1], ALU.add, ALU.max).then_inc(s_o, 1)

            def exponents(s):
                if s.live(WKV_LAG):
                    dve.wait_ge(s_o, s.count(WKV_LAG, M, M))
                    dve.wait_ge(s_relu, s.count(WKV_LAG, 2 * M))
                    V.tensor_tensor(rel[:, :, :], opq[:, O, :, 0:TN], kv[:, 0, :, :],
                                    ALU.subtract).then_inc(s_rel, 1)
                    dve.wait_ge(s_rel, s.count(WKV_LAG, 1, 1))
                    for kind, op in ((STATE_W, ALU.min), (TOKEN_W, ALU.max)):
                        for m in range(M):
                            V.tensor_scalar(ex[:, kind, m, :], rel[:, m, :], decay[:, m:m + 1], 0.0, ALU.add,
                                            op).then_inc(s_arg, 1)

            def recurrences(s):
                if s.live(WKV_LAG):
                    dve.wait_ge(s_ex, s.count(WKV_LAG, 3, 2))
                    dve.wait_ge(s_st[0], s.count(0, M, M))
                    dve.wait_ge(s_kv, s.count(WKV_LAG, 2 * M, 2 * M))
                    V.tensor_tensor(b2v[:, :, :], ex[:, TOKEN_W, :, :], kv[:, 1, :, :], ALU.mult).then_inc(s_b2v, 1)
                    for m in range(M):
                        V.tensor_tensor_scan(opq[:, Q, m, 1:1 + TN], ex[:, STATE_W, m, :], ex[:, TOKEN_W, m, :],
                                             opq[:, Q, m, 0:1], ALU.mult, ALU.add).then_inc(s_q, 1)
                    dve.wait_ge(s_b2v, s.count(WKV_LAG, 1, 1))
                    for m in range(M):
                        V.tensor_tensor_scan(opq[:, PN, m, 1:1 + TN], ex[:, STATE_W, m, :], b2v[:, m, :],
                                             opq[:, PN, m, 0:1], ALU.mult, ALU.add).then_inc(s_p, 1)

            def gate_state(s, halves=range(2)):
                if s.live(OUT_LAG):
                    if is_last(s, OUT_LAG):
                        dve.wait_ge(s_relu, 2 * M * NT)
                    else:
                        dve.wait_ge(s_add, s.count(OUT_LAG, 1))
                    for h in halves:
                        dve.wait_ge(s_ot, s.count(OUT_LAG, 2, h + 1))
                        V.scalar_tensor_tensor(out=gate_of(s)[:, 2 * h:2 * h + 2, :],
                                               in0=o_tanh_of(s)[:, 2 * h:2 * h + 2, :],
                                               scalar=1.0, in1=turned_tile(s)[:, 2 * h:2 * h + 2, :], op0=ALU.add,
                                               op1=ALU.mult).then_inc(s_gate, 1)

            def denominator(s):
                if s.live(WKV_LAG):
                    dve.wait_ge(s_ex, s.count(WKV_LAG, 3, 3))
                    dve.wait_ge(s_q, s.count(WKV_LAG, M, M))
                    dve.wait_ge(s_ln, s.count(WKV_LAG, 1))
                    V.tensor_tensor(den[:, :, :], ex[:, STATE_Y, :, :], opq[:, Q, :, 0:TN],
                                    ALU.mult).then_inc(s_aq, 1)
                    dve.wait_ge(s_p, s.count(WKV_LAG, M, M))
                    dve.wait_ge(s_numr, s.count(WKV_LAG, 1))
                    V.tensor_tensor(num[:, :, :], ex[:, STATE_Y, :, :], opq[:, PN, :, 0:TN],
                                    ALU.mult).then_inc(s_ap, 1)
                    dve.wait_ge(s_aq, s.count(WKV_LAG, 1, 1))
                    V.tensor_tensor(den[:, :, :], ex[:, TOKEN_Y, :, :], den[:, :, :], ALU.add).then_inc(s_den, 1)

            def numerator(s):
                if s.live(WKV_LAG):
                    V.tensor_tensor(b2v[:, :, :], ex[:, TOKEN_Y, :, :], kv[:, 1, :, :], ALU.mult).then_inc(s_bv, 1)
                    dve.wait_ge(s_ap, s.count(WKV_LAG, 1, 1))
                    V.tensor_copy(opq[:, :, :, 0:1], opq[:, :, :, TN:TN + 1]).then_inc(s_carry, 1)
                    dve.wait_ge(s_bv, s.count(WKV_LAG, 1, 1))
                    V.tensor_tensor(num[:, :, :], num[:, :, :], b2v[:, :, :], ALU.add).then_inc(s_num, 1)

            def wkv_output(s):
                if s.live(Y_LAG):
                    dve.wait_ge(s_rec, s.count(Y_LAG, 1, 1))
                    dve.wait_ge(s_numr, s.count(Y_LAG, 1, 1))
                    if not is_last(s, Y_LAG):
                        dve.wait_ge(s_proj, s.count(Y_LAG, 2))
                    V.tensor_tensor(wkv_of(s, Y_LAG)[:, :, :], num_r[:, :, :],
                                    reciprocal_of(s)[:, :, :], ALU.mult).then_inc(s_y, 1)

            def times_r(s):
                if s.live(WKV_LAG):
                    dve.wait_ge(s_num, s.count(WKV_LAG, 1, 1))
                    dve.wait_ge(s_rt, s.count(WKV_LAG, 1, 1))
                    if s.live(Y_LAG):
                        dve.wait_ge(s_y, s.count(Y_LAG, 1, 1))
                    V.scalar_tensor_tensor(out=num_r[:, :, :], in0=r_tanh[:, :, :], scalar=1.0, in1=num[:, :, :],
                                           op0=ALU.add, op1=ALU.mult).then_inc(s_numr, 1)

            def gated(s, h):
                if s.live(OUT_LAG):
                    dve.wait_ge(s_gate, s.count(OUT_LAG, 2, h + 1))
                    dve.wait_ge(s_proj, s.count(OUT_LAG, 2, h + 1))
                    V.tensor_tensor(gate_of(s)[:, 2 * h:2 * h + 2, :], projected_tile(s)[:, 2 * h:2 * h + 2, :],
                                    gate_of(s)[:, 2 * h:2 * h + 2, :], ALU.mult).then_inc(s_z, 1)

            def slot_body(s):
                update(s, 2)
                update(s, 1)
                maxima(s)
                exponents(s)
                split_xt(s)
                update(s, 0)
                mix(s)
                recurrences(s)
                gate_state(s)
                denominator(s)
                if s.live(NET_LAG[0]):
                    numerator(s)
                    wkv_output(s)
                    for h in range(2):
                        gated(s, h)
                    split_r(s)
                else:
                    for h in range(2):
                        gated(s, h)
                    wkv_output(s)
                    numerator(s)
                times_r(s)

            def drain(a, b, c):
                update(a, 2)
                update(a, 1)
                maxima(a)
                exponents(a)
                update(a, 0)
                recurrences(a)
                denominator(a)
                gate_state(a)
                update(b, 1)
                wkv_output(a)
                for h in range(2):
                    gated(a, h)
                numerator(a)
                times_r(a)
                update(b, 2)
                wkv_output(b)
                gate_state(b)
                gated(b, 0)
                for h in range(2):
                    half = half_tile(h)
                    dve.wait_ge(s_cs[2], NT + h)
                    dve.wait_ge(s_st[1], M * NT)
                    V.tensor_tensor(turned[0][:, :, half], coup[2][:, half].unsqueeze(1).to_broadcast(
                        [P, M, TN // 2]), h1[0][:, :, half], ALU.mult).then_inc(s_mul[2], 1)
                    dve.wait_ge(s_mul[2], NT + h)
                    dve.wait_ge(s_tp, 2 * (NT - 1))
                    V.tensor_tensor(state[2][:, 0, half], h1[0][:, 0, half], turned[0][:, 1, half],
                                    ALU.add).then_inc(s_st[2], 1)
                    V.tensor_tensor(state[2][:, 1, half], h1[0][:, 1, half], turned[0][:, 0, half],
                                    ALU.subtract).then_inc(s_st[2], 1)
                gated(b, 1)
                dve.wait_ge(s_xl, 16)
                gate_state(c, (0,))
                gated(c, 0)
                gate_state(c, (1,))
                gated(c, 1)
                for h in range(2):
                    dve.wait_ge(s_z, 2 * (NT - 1) + h + 1)
                    V.tensor_tensor(last_resid[:, 2 * h:2 * h + 2, :], gate_of(c)[:, 2 * h:2 * h + 2, :],
                                    last_resid[:, 2 * h:2 * h + 2, :], ALU.add).then_inc(s_last, 1)
            run_slots(dve, slot_body, drain)

        @block.tensor
        def _(pe):
            mm = nc.tensor.matmul
            pe.wait_ge(s_ident, 1)
            with pe.Fori(0, WARM_UP):
                for m in range(M):
                    for k in range(SUB):
                        nc.tensor.transpose(ps[:, KVR_BANK + m, k * P:(k + 1) * P], ident[:, :], ident[:, :])

            def layer1(c, round_start, src, ready=None):
                if ready:
                    pe.wait_ge(*ready)
                pe.wait_ge(s_th[c], round_start(c, 1, 0))
                for m in range(M):
                    for k in range(M):
                        last = mm(ps[:, 2 * c + m, :], w_c1[:, k, m * P:(m + 1) * P], src[:, k, :],
                                  start=(k == 0), stop=(k == M - 1))
                    last.then_inc(s_h1[c], 1)

            def split_products(dst, weights, source, columns):
                products = [(k, w, x) for w, x in ((1, 0), (0, 1), (0, 0)) for k in range(M)]
                for i, (k, w, x) in enumerate(products):
                    last = mm(dst, weights[w][:, k, columns], source[x][:, k, :], start=(i == 0),
                              stop=(i == len(products) - 1))
                return last

            def layer1_split(c, round_start, splits):
                pe.wait_ge(s_split, splits)
                pe.wait_ge(s_th[c], round_start(c, 1, 0))
                for m in range(M):
                    split_products(ps[:, 2 * c + m, :], w_c1_split, xt_split, slice(m * P, (m + 1) * P)
                                   ).then_inc(s_h1[c], 1)

            def layer2(c, round_start):
                pe.wait_ge(s_g1[c], round_start(c, M, M))
                for k in range(M):
                    last = mm(ps[:, 2 * c, :], w_c2[:, k, :], h1[c][:, k, :], start=(k == 0), stop=(k == M - 1))
                last.then_inc(s_h2[c], 1)

            def layer3(c, round_start):
                pe.wait_ge(s_g2[c], round_start(c, 1, 1))
                mm(ps[0:D3, 2 * c + 1, :], w_c3[:, :], h2[c], start=True, stop=True).then_inc(s_h3[c], 1)

            def logits(c, round_start):
                pe.wait_ge(s_g3[c], round_start(c, 1, 1))
                mm(ps[:, 2 * c, :], w_c4[0:D3, :], h3[c][0:D3, :], start=True, stop=True).then_inc(s_lg[c], 1)

            def prologue_round(c, per_round, k):
                return k

            def prologue_net(step):
                for layer, t in PROLOGUE_NET.get(step, ()):
                    if layer == 0:
                        layer1(t, prologue_round, prologue_cols(t), (s_xe, M * (t + 1)))
                    else:
                        (layer2, layer3)[layer - 1](t, prologue_round)

            for g in range(NT):
                pe.wait_ge(s_xn_v, g + 1)
                pe.wait_ge(s_xn_p, g + 1)
                pe.wait_ge(s_xn_s, 2 * (g + 1))
                for m in range(M):
                    if g >= 1:
                        pe.wait_ge(s_xe, M * (g - 1) + m + 1)
                    for k in range(SUB):
                        last = nc.tensor.transpose(ps[:, KVR_BANK + m, k * P:(k + 1) * P],
                                                   xn_stage[:, g % 2, k, m * P:(m + 1) * P], ident[:, :])
                    last.then_inc(s_xt, 1)
                if g == 1:
                    pe.wait_ge(s_wc, 16 * 4)
                prologue_net(g)
            def project(s, w, m):
                pe.wait_ge(s_mix, s.count(WKV_LAG, 3 * M, M * (w + 1)))
                if w == 0:
                    pe.wait_ge(s_z, s.count(OUT_LAG, 2))
                else:
                    pe.wait_ge(s_kv, s.count(WKV_LAG, 2 * M, M * (w - 1) + m + 1))
                out_bank, columns = ps[:, KVR_BANK + m, :], slice(m * P, (m + 1) * P)
                if w == 2 and splits_r(s, WKV_LAG):
                    pe.wait_ge(s_rsplit, s.count(WKV_LAG, 2, 4))
                    last = split_products(out_bank, w_r_split, mixed_r_split, columns)
                else:
                    for k in range(M):
                        last = mm(out_bank, w_kvr[:, w, k, columns], mixed[:, w, k, :],
                                  start=(k == 0), stop=(k == M - 1))
                last.then_inc(s_kvr, 1)

            pe.wait_ge(s_wg, 16 * 3)
            pe.wait_ge(s_wt, 16 * 4)
            pe.wait_ge(s_xe, M * NT)
            logits(0, prologue_round)
            pe.wait_ge(s_mean, 1)
            for m in range(M):
                last = mm(ps[:, GLOBAL_BANK, 0:1], w_g1[:, m, :], ctx_mean[:, m:m + 1], start=(m == 0),
                          stop=(m == 1))
            last.then_inc(s_gp, 1)
            logits(2, prologue_round)
            pe.wait_ge(s_ga, 1)
            mm(ps[0:D3, GLOBAL_BANK, 1:2], w_g2[:, :], g_h1[:, :], start=True, stop=True).then_inc(s_gp, 1)
            project(Slot(NT, 0), 0, 0)
            pe.wait_ge(s_ga, 2)
            mm(ps[:, GLOBAL_BANK, 2:3], w_g3[0:D3, :], g_h2[0:D3, :], start=True, stop=True).then_inc(s_gp, 1)
            project(Slot(NT, 0), 0, 1)
            pe.wait_ge(s_ga, 3)
            logits(1, prologue_round)
            pe.wait_ge(s_const, 8)

            def turn_state(s, halves=range(2)):
                if s.live(OUT_LAG):
                    pe.wait_ge(s_st[2], s.count(OUT_LAG, M, M))
                    if is_last(s, OUT_LAG):
                        pe.wait_ge(s_th[1], last_round(1, 1, 1))
                    elif not s.live(NET_LAG[0]):
                        pe.wait_ge(s_th[0], NT - AHEAD + 1)
                    for h in halves:
                        if s.live(NET_LAG[0]):
                            pe.wait_ge(s_r, s.count(WKV_LAG, M, h + 1))
                            pe.wait_ge(s_z, s.count(OUT_LAG, 2))
                        if not is_last(s, OUT_LAG):
                            pe.wait_ge(s_gate, s.count(OUT_LAG, 2))
                        elif h:
                            pe.wait_ge(s_st[2], M * (NT + 1))
                        for k in (2 * h, 2 * h + 1):
                            for m in range(M):
                                last = nc.tensor.transpose(turned_tile(s)[:, k, m * P:(m + 1) * P],
                                                           state[2][:, m, k * P:(k + 1) * P], ident[:, :])
                        last.then_inc(s_tp, 1)

            def project_out(s, h, parts=range(2)):
                if s.live(OUT_LAG):
                    src, dst = wkv_of(s, OUT_LAG), projected_tile(s)
                    pe.wait_ge(s_y, s.count(OUT_LAG, 1, 1))
                    if is_last(s, OUT_LAG):
                        pe.wait_ge(s_th[2], NT)
                    elif s.live(NET_LAG[0]):
                        pe.wait_ge(s_gate, s.count(OUT_LAG, 2, h + 1))
                    else:
                        pe.wait_ge(s_r, s.count(WKV_LAG, M, h + 1))
                        pe.wait_ge(s_z, s.count(OUT_LAG, 2))
                    for k in [2 * h + part for part in parts]:
                        for m in range(M):
                            last = mm(dst[:, k, :], src[:, m, k * P:(k + 1) * P], w_o[:, m, :],
                                      start=(m == 0), stop=(m == M - 1))
                    if 1 in parts:
                        last.then_inc(s_proj, 1)

            def slot_body(s):
                nets = [c for c in NET_ORDER if s.live(NET_LAG[c])]
                if s.live(WKV_LAG):
                    for w in range(3):
                        for m in range(M):
                            if s.base > 0 or w > 0:
                                project(s, w, m)
                if 2 in nets:
                    layer1(2, s.round, state[1], (s_st[1], s.count(1, M, M)))
                if 0 in nets:
                    layer1_split(0, s.round, s.round(0, 2, 2))
                turn_state(s)
                if not s.live(NET_LAG[0]):
                    project_out(s, 0)
                    project_out(s, 1)
                if 1 in nets:
                    layer1(1, s.round, state[0], (s_st[0], s.count(0, M, M)))
                for c in nets:
                    layer2(c, s.round)
                if s.live(NET_LAG[0]):
                    project_out(s, 0)
                    project_out(s, 1)
                for layer in (layer3, logits):
                    for c in nets:
                        layer(c, s.round)

            def drain(a, b, c):
                for w in range(3):
                    for m in range(M):
                        project(a, w, m)
                layer1(2, a.round, state[1], (s_st[1], a.count(1, M, M)))
                turn_state(a)
                layer1(1, a.round, state[0], (s_st[0], a.count(0, M, M)))
                project_out(a, 0)
                layer2(1, a.round)
                project_out(a, 1, (0,))
                layer3(1, a.round)
                layer2(2, a.round)
                logits(1, a.round)
                project_out(a, 1, (1,))
                layer3(2, a.round)
                logits(2, a.round)
                layer1(1, last_round, h1[0], (s_st[1], M * NT))
                project_out(b, 0)
                layer2(1, last_round)
                project_out(b, 1, (0,))
                layer3(1, last_round)
                turn_state(b)
                logits(1, last_round)
                project_out(b, 1, (1,))
                project_out(c, 0)
                turn_state(c, (0,))
                project_out(c, 1)
                turn_state(c, (1,))
            run_slots(pe, slot_body, drain)


def kernel(**inputs):
    import numpy as np
    import concourse.bacc as bacc
    from concourse import mybir as _mybir
    from concourse.bass_utils import run_bass_kernel_spmd as run

    a = {k: np.asarray(v) for k, v in inputs.items()}
    x = a["L0_attn_x"]
    T, C = x.shape[1:]

    def chunks(v):
        return np.ascontiguousarray(v.reshape(-1, P).T)

    vec = np.zeros((P, NVEC), np.float32)
    vec[:, DECAY:DECAY + 2] = chunks(a["L0_attn_time_decay"])
    vec[:, FIRST:FIRST + 2] = chunks(a["L0_attn_time_first"])
    for i, n in enumerate("kvr"):
        vec[:, MIX + 2 * i:MIX + 2 * i + 2] = chunks(a[f"L0_attn_time_mix_{n}"])
    vec[:, CN_B1:CN_B1 + 2] = chunks(a["L0_ffn_cn_b1"])
    vec[:, CN_B2] = a["L0_ffn_cn_b2"]
    vec[0:64, CN_B3] = a["L0_ffn_cn_b3"]
    vec[:, CN_B4] = a["L0_ffn_cn_b4"]
    vec[:, GC_B1] = a["L0_ffn_gc_b1"]
    vec[0:64, GC_B2] = a["L0_ffn_gc_b2"]
    vec[:, GC_B3] = a["L0_ffn_gc_b3"]
    vec[:, RANGE] = a["L0_ffn_adaptive_range"]
    vec[0:64, SIGN] = 1.0
    vec[64:P, SIGN] = -1.0

    arrays = {
        "x": x.reshape(T, C), "vec": vec,
        "wk_t": a["L0_attn_Wk"].T, "wv_t": a["L0_attn_Wv"].T, "wr_t": a["L0_attn_Wr"].T, "wo_t": a["L0_attn_Wo"].T,
        "cn_w1": a["L0_ffn_cn_w1"], "cn_w2": a["L0_ffn_cn_w2"], "cn_w3": a["L0_ffn_cn_w3"],
        "cn_w4": np.repeat(a["L0_ffn_cn_w4"], P, axis=1),
        "gc_w1": a["L0_ffn_gc_w1"], "gc_w2": a["L0_ffn_gc_w2"],
        "gc_w3": np.repeat(a["L0_ffn_gc_w3"], P, axis=1),
    }
    arrays = {k: np.ascontiguousarray(v) for k, v in arrays.items()}
    nc = bacc.Bacc("TRN2", target_bir_lowering=False, num_devices=1)
    args = [nc.dram_tensor(k, v.shape, _mybir.dt.from_np(v.dtype), kind="ExternalInput").ap()
            for k, v in arrays.items()]
    out = nc.dram_tensor("out", (T, C), F32, kind="ExternalOutput").ap()
    rwkv_coupled_ffn(nc, *args, out)
    r = run(nc, [arrays], core_ids=[0])
    return r.results[0]["out"].reshape(1, T, C)
```
